# Optimizing a Trainium2 kernel written in Bass

```python
import numpy as np
import jax
import jax.numpy as jnp

def _softmax(x, axis=-1):
    return jax.nn.softmax(x, axis=axis)

def _gelu(x):
    return jax.nn.gelu(x, approximate=True)

def _silu(x):
    return jax.nn.silu(x)

def _sigmoid(x):
    return jax.nn.sigmoid(x)

def _layernorm(x, axis=-1, eps=1e-05):
    m = jnp.mean(x, axis=axis, keepdims=True)
    v = jnp.var(x, axis=axis, keepdims=True)
    return (x - m) / jnp.sqrt(v + eps)

def _scatter_add(tgt, idx, src, axis=0):
    return tgt.at[idx].add(src)

def _segment_sum(src, seg, n):
    return jax.ops.segment_sum(src, seg, n)
kernel_name = 'mk_adj_preln_d1_adj_r2_b22382'

def setup_inputs(seed: int=0):
    np.random.seed(seed)
    _w = jnp.asarray

    def _rec_inputs():
        import jax
        import jax.numpy as jnp
        _gk = jax.random.key(seed)
        x = -0.0005963 + 1.001 * jax.random.normal(jax.random.fold_in(_gk, 1), (2048, 256), jnp.float32)
        _a = jax.random.bernoulli(jax.random.fold_in(_gk, 2), 0.0078125, (2048, 2048))
        _a = jnp.logical_or(_a, jnp.swapaxes(_a, -1, -2))
        _a = jnp.logical_or(_a, jnp.eye(2048, dtype=bool))
        _af = _a.astype(jnp.float32)
        adj = _af
        return (x, adj)
    x, adj = _rec_inputs()

    def _L0_gnn_setup():
        import jax, jax.numpy as jnp
        import numpy as np
        N = 3072
        D_IN = 256
        D_OUT = 256
        DENSITY = 0.005
        key = jax.random.key(seed)
        ks = jax.random.split(key, 12)
        x = jax.random.normal(ks[0], (N, D_IN), dtype=jnp.float32)
        adj_a = (jax.random.uniform(ks[1], (N, N)) < DENSITY).astype(jnp.float32)
        adj_b = (jax.random.uniform(ks[2], (N, N)) < DENSITY).astype(jnp.float32)
        W_sa = jax.random.normal(ks[3], (D_IN, D_OUT), dtype=jnp.float32) * (1.414 / np.sqrt(D_IN + D_OUT))
        a_sa = jax.random.normal(ks[4], (1, 2 * D_OUT), dtype=jnp.float32) * (1.414 / np.sqrt(1 + 2 * D_OUT))
        stdv = 1.0 / np.sqrt(D_OUT)
        W_gcnb = jax.random.uniform(ks[5], (D_IN, D_OUT), minval=-stdv, maxval=stdv, dtype=jnp.float32)
        b_gcnb = jax.random.uniform(ks[6], (D_OUT,), minval=-stdv, maxval=stdv, dtype=jnp.float32)
        s = 1.0 / np.sqrt(2 * D_IN)
        Wa = jax.random.uniform(ks[7], (1, 2 * D_IN), minval=-s, maxval=s, dtype=jnp.float32)
        ba = jax.random.uniform(ks[8], (1,), minval=-s, maxval=s, dtype=jnp.float32)
        Wb = jax.random.uniform(ks[9], (1, 2 * D_IN), minval=-s, maxval=s, dtype=jnp.float32)
        bb = jax.random.uniform(ks[10], (1,), minval=-s, maxval=s, dtype=jnp.float32)
        return {'x': x, 'adj_a': adj_a, 'adj_b': adj_b, 'W_sa': W_sa, 'a_sa': a_sa, 'W_gcnb': W_gcnb, 'b_gcnb': b_gcnb, 'Wa': Wa, 'ba': ba, 'Wb': Wb, 'bb': bb}
    _L0_gnn_all = _L0_gnn_setup()
    _L0_gnn_in = {k: v for k, v in _L0_gnn_all.items() if k in ('W_sa', 'a_sa', 'W_gcnb', 'b_gcnb', 'Wa', 'ba', 'Wb', 'bb')}
    del _L0_gnn_all
    return {'x': x, 'adj': adj, 'L0_gnn_W_sa': _L0_gnn_in['W_sa'], 'L0_gnn_a_sa': _L0_gnn_in['a_sa'], 'L0_gnn_W_gcnb': _L0_gnn_in['W_gcnb'], 'L0_gnn_b_gcnb': _L0_gnn_in['b_gcnb'], 'L0_gnn_Wa': _L0_gnn_in['Wa'], 'L0_gnn_ba': _L0_gnn_in['ba'], 'L0_gnn_Wb': _L0_gnn_in['Wb'], 'L0_gnn_bb': _L0_gnn_in['bb']}

def reference(x, adj, L0_gnn_W_sa, L0_gnn_a_sa, L0_gnn_W_gcnb, L0_gnn_b_gcnb, L0_gnn_Wa, L0_gnn_ba, L0_gnn_Wb, L0_gnn_bb):
    import jax
    import jax.numpy as jnp

    def _L0_gnn_ref(x, adj_a, adj_b, W_sa, a_sa, W_gcnb, b_gcnb, Wa, ba, Wb, bb):
        import jax, jax.numpy as jnp
        import numpy as np
        N = 3072
        D_IN = 256
        D_OUT = 256
        DENSITY = 0.005
        type_sum_a = adj_a @ x
        type_sum_b = adj_b @ x
        attn_a = jax.nn.sigmoid(jnp.concatenate([type_sum_a, x], axis=1) @ Wa.T + ba)
        attn_b = jax.nn.sigmoid(jnp.concatenate([type_sum_b, x], axis=1) @ Wb.T + bb)
        h = x @ W_sa
        Hd = h.shape[1]
        s_left = h @ a_sa[0, :Hd]
        s_right = h @ a_sa[0, Hd:]
        scores = s_left[:, None] + s_right[None, :]
        e = jnp.where(adj_a != 0, jnp.exp(-jax.nn.leaky_relu(scores, 0.01)), 0.0)
        attn = e / (jnp.sum(e, axis=1, keepdims=True) + 1e-05)
        x_a = attn @ h
        x_b = adj_b @ (x @ W_gcnb) + b_gcnb
        return jax.nn.sigmoid(attn_a * x_a + attn_b * x_b)
    h = jnp.maximum(_layernorm(x, axis=-1), 0.0)
    x = x + _L0_gnn_ref(h, adj, adj, L0_gnn_W_sa, L0_gnn_a_sa, L0_gnn_W_gcnb, L0_gnn_b_gcnb, L0_gnn_Wa, L0_gnn_ba, L0_gnn_Wb, L0_gnn_bb)
    return x

_drawn_inputs = setup_inputs


def setup_inputs(seed=0):
    import zlib

    import numpy as np

    out = dict(_drawn_inputs(seed))
    spreads = {}
    factors = {'L0_gnn_W_sa': 22.263, 'L0_gnn_a_sa': 40.735, 'L0_gnn_b_gcnb': 46.802, 'L0_gnn_Wa': 4.748}
    for name, (base, spread) in spreads.items():
        noise = np.random.default_rng([zlib.crc32(name.encode()), seed]).standard_normal(out[name].shape)
        drawn = base * np.exp(spread * noise) if base else spread * noise
        out[name] = jnp.asarray(drawn.astype(out[name].dtype))
    for name, factor in factors.items():
        out[name] = (out[name] * factor).astype(out[name].dtype)
    return out
```

```python
import concourse.bass as bass
from concourse import mybir
from contextlib import ExitStack

P = 128


def graph_layer(nc, x, adj, w_sa, a_sa, w_gcnb, b_gcnb, wa, ba, wb, bb, out):
    f32, f32r = mybir.dt.float32, mybir.dt.float32r
    bf16, u16 = mybir.dt.bfloat16, mybir.dt.uint16
    ALU, ACT = mybir.AluOpType, mybir.ActivationFunctionType

    N, D = x.shape
    LN_EPS, DEN_EPS, SLOPE = 1e-5, 1e-5, 0.01
    DC = D // P
    JB = N // P
    GROUP = 4
    GROUPS = JB // GROUP
    GW = GROUP * P
    RB = 2
    ROWS = RB * P
    BLOCKS = N // ROWS
    TB = 2
    TW = TB * P
    TILES = N // TW
    LOAD = 2
    LOADS = TILES // LOAD
    SUM = D + 2
    GATE = D
    SELF = D + 2
    RIGHT99, RIGHT01, LEFT = 2, 3, 4
    OWN = 6
    CAT = SELF + OWN
    CLEAR_AHEAD = 2
    RING = 4
    ERING = 4
    STAGE_AHEAD = 4
    TAKE = 2
    MIX = TAKE + 1
    STORE = 6
    UNIT_BANKS = 3
    SPLIT = GROUP // 2
    assert TILES % RING == 0 and TAKE < RING and N == BLOCKS * ROWS

    with ExitStack() as ctx:
        def sb(name, shape, dt=f32):
            return ctx.enter_context(nc.sbuf_tensor(name, [P] + shape, dt))

        def sem(name):
            return ctx.enter_context(nc.semaphore(name))

        W_LOADS, BIAS_LOADS = 3, 3
        ident = sb("ident", [P])
        ident_b = sb("ident_b", [P], bf16)
        x_sb = sb("x_sb", [JB, D])
        stats = sb("stats", [JB, 6])
        mean_var = sb("mean_var", [JB, 2])
        std = sb("std", [JB])
        rstd = sb("rstd", [JB])
        neg_mean_rstd = sb("neg_mean_rstd", [JB])
        warm = sb("warm", [1])
        xn = sb("xn", [2, GROUP, D])
        hnT_hi = sb("hnT_hi", [2, DC, GW], f32r)
        hnT_lo = sb("hnT_lo", [2, DC, GW], f32r)
        w_sa_sb = sb("w_sa_sb", [DC, D])
        w_sa_hi = sb("w_sa_hi", [DC, D], f32r)
        w_sa_lo = sb("w_sa_lo", [DC, D], f32r)
        w_cat = sb("w_cat", [DC, CAT])
        w_cat_hi = sb("w_cat_hi", [DC, CAT], f32r)
        w_cat_lo = sb("w_cat_lo", [DC, CAT], f32r)
        gate_rows = sb("gate_rows", [D])
        a_all = sb("a_all", [2 * D])
        b_all = sb("b_all", [SUM])
        own_bias = sb("own_bias", [OWN])
        dot_junk = sb("dot_junk", [D])
        neg_v = sb("neg_v", [DC, 2])
        neg_sl = sb("neg_sl", [N])
        neg_sl01 = sb("neg_sl01", [N])
        own = sb("own", [JB, OWN])
        g_hi = sb("g_hi", [JB, SUM], f32r)
        g_lo = sb("g_lo", [JB, SUM], f32r)
        h_hi = sb("h_hi", [JB, SUM], f32r)
        h_lo = sb("h_lo", [JB, D], f32r)

        adj_sb = sb("adj_sb", [LOADS, RB, LOAD * TW])
        score = sb("score", [RING, TB, ROWS])
        e = sb("e", [ERING, TB, ROWS])
        adjT = sb("adjT", [RING, TB, ROWS], f32r)
        e_hi = sb("e_hi", [RING, TB, ROWS], f32r)
        e_lo = sb("e_lo", [RING, TB, ROWS], f32r)

        conv = sb("conv", [RB, SUM])
        att_sum = sb("att_sum", [RB, SUM])
        logit = sb("logit", [RB, 2])
        exp_neg = sb("exp_neg", [RB, 2])
        one_plus = sb("one_plus", [RB, 2])
        gate = sb("gate", [RB, 2])
        den = sb("den", [RB])
        inv_den = sb("inv_den", [RB])
        att_scale = sb("att_scale", [RB])
        att = sb("att", [RB, D])
        mixed = sb("mixed", [RB, D])
        sig = sb("sig", [RB, D])
        y = sb("y", [RB, D])

        bank = [ctx.enter_context(nc.psum_tensor(f"bank{i}", [P, 512], f32)) for i in range(8)]
        adj_acc, att_acc = bank[0:RB], bank[RB:2 * RB]
        staged = [bank[4 + i][:, :].bitcast(bf16)[:, 0:TB * ROWS].rearrange("p (b r) -> p b r", b=TB)
                  for i in range(RING)]
        adj_b = adj_sb[:, :, :, :].bitcast(bf16).rearrange("p q r (j two) -> p q r j two", two=2)[:, :, :, :, 1]

        x_loaded = [sem(f"x_loaded{g}") for g in range(GROUPS)]
        w_loaded = sem("w_loaded")
        bias_loaded = sem("bias_loaded")
        rows_loaded = sem("rows_loaded")
        adj_loaded = [sem(f"adj_loaded{q}") for q in range(LOADS)]
        ident_cleared = sem("ident_cleared")
        ident_ready = sem("ident_ready")
        ident_b_ready = sem("ident_b_ready")
        consts_ready = sem("consts_ready")
        dve_steps = sem("dve_steps")
        var_ready = sem("var_ready")
        std_ready = sem("std_ready")
        rstd_ready = sem("rstd_ready")
        xn_ready = sem("xn_ready")
        gate_cols_ready = sem("gate_cols_ready")
        w_cat_ready = sem("w_cat_ready")
        w_hi_ready = sem("w_hi_ready")
        w_lo_ready = sem("w_lo_ready")
        xn_transposed = sem("xn_transposed")
        hnT_hi_ready = sem("hnT_hi_ready")
        hnT_lo_ready = sem("hnT_lo_ready")
        unit_done = sem("unit_done")
        unit_hi_taken = sem("unit_hi_taken")
        unit_lo_taken = sem("unit_lo_taken")
        sl_spread = sem("sl_spread")
        sl_taken = sem("sl_taken")

        arg_ready = sem("arg_ready")
        exp_ready = sem("exp_ready")
        e_zeroed = sem("e_zeroed")
        tile_transposed = sem("tile_transposed")
        adjT_ready = sem("adjT_ready")
        e_ready = sem("e_ready")
        e_hi_ready = sem("e_hi_ready")
        e_lo_ready = sem("e_lo_ready")
        tile_summed = sem("tile_summed")
        rows_summed = [sem(f"rows_summed{r}") for r in range(RB - 1)]
        conv_ready = [sem(f"conv_ready{r}") for r in range(RB)]
        att_sum_ready = [sem(f"att_sum_ready{r}") for r in range(RB)]
        logit_ready = sem("logit_ready")
        exp_neg_ready = sem("exp_neg_ready")
        den_ready = sem("den_ready")
        inv_den_ready = sem("inv_den_ready")
        one_plus_ready = sem("one_plus_ready")
        gate_ready = sem("gate_ready")
        att_scale_ready = sem("att_scale_ready")
        att_ready = sem("att_ready")
        mixed_ready = sem("mixed_ready")
        tanh_ready = sem("tanh_ready")
        sig_ready = sem("sig_ready")
        y_ready = sem("y_ready")
        stored = sem("stored")

        ALL_UNITS = 2 * JB

        def later(s):
            return not isinstance(s, int) or s > 0

        def apart(engine, value):
            value = value if isinstance(value, int) else engine.to_reg(value)
            engine.wait_ge(ident_ready, 1)
            return value

        def body(s, ahead):
            return [(s, t) for t in range(ahead, TILES)] + [(s + 1, t) for t in range(ahead)]

        def ahead_of(s, t, k):
            return (s, t + k) if t + k < TILES else (s + 1, t + k - TILES)

        def ended(s, t):
            return isinstance(s, int) and s >= BLOCKS

        def wait_rows_summed(engine, s, r):
            if r < RB - 1:
                engine.wait_ge(rows_summed[r], s + 1)
            else:
                engine.wait_ge(tile_summed, TILES * (s + 1))

        x_rows = x.rearrange("(g b p) d -> g p b d", p=P, b=GROUP)
        adj_rows = adj.rearrange("(s r p) j -> s p r j", p=P, r=RB)
        out_rows = out.rearrange("(s r p) d -> s p r d", p=P, r=RB)

        block = ctx.enter_context(nc.Block())

        @block.sync
        def _(sp):
            def load_x(g):
                sp.dma_start(x_sb[:, g * GROUP:(g + 1) * GROUP, :], x_rows[g]).then_inc(x_loaded[g], 16)

            load_x(0)
            sp.dma_start(w_sa_sb[:, :, :], w_sa.rearrange("(c p) n -> p c n", p=P)).then_inc(w_loaded, 16)
            sp.dma_start(a_all[:, :], a_sa.broadcast_to([P, 2 * D])).then_inc(w_loaded, 16)
            load_x(1)
            sp.dma_start(w_cat[:, :, 0:D], w_gcnb.rearrange("(c p) n -> p c n", p=P)).then_inc(w_loaded, 16)
            for g in range(2, GROUPS):
                load_x(g)

            def load(s, q):
                cols = slice(q * LOAD * TW, (q + 1) * LOAD * TW)
                sp.dma_start(adj_sb[:, q, :, :], adj_rows[s, :, :, cols]).then_inc(adj_loaded[q], 16)

            def store(s):
                sp.wait_ge(y_ready, s + 1)
                sp.dma_start(out_rows[s], y[:, :, :]).then_inc(stored, 16)

            def load_block(s):
                for q in range(LOADS):
                    sp.wait_ge(tile_transposed, TILES * (s - 1) + LOAD * (q + 1))
                    load(s, q)

            for q in range(LOADS):
                load(0, q)
            load_block(1)
            with sp.Fori(2, BLOCKS) as s:
                load_block(s)
                store(s - 2)
            store(BLOCKS - 2)
            store(BLOCKS - 1)
            sp.wait_ge(stored, 16 * BLOCKS)

        @block.gpsimd
        def _(pool):
            nc.gpsimd.memset(ident[:, :], 0.0).then_inc(ident_cleared, 1)
            pool.wait_ge(ident_cleared, 1)
            nc.gpsimd.affine_select(out=ident[:, :], in_=ident[:, :], compare_op=ALU.not_equal, fill=1.0,
                                    base=0, pattern=[[-1, P]], channel_multiplier=1).then_inc(ident_ready, 1)
            nc.gpsimd.memset(h_hi[:, :, D:D + 1].bitcast(f32), 1.0)
            nc.gpsimd.memset(h_hi[:, :, D + 1:SUM].bitcast(f32), 0.0)
            nc.gpsimd.memset(b_all[:, D:SUM], 0.0)
            nc.gpsimd.memset(w_cat[:, :, CAT - 1:CAT], 0.0)
            nc.gpsimd.memset(own_bias[:, 2:OWN], 0.0).then_inc(consts_ready, 1)
            pool.wait_ge(ident_ready, 1)
            nc.gpsimd.tensor_copy(ident_b[:, :], ident[:, :]).then_inc(ident_b_ready, 1)

            def normalise(g):
                pool.wait_ge(rstd_ready, g + 1)
                pool.wait_ge(xn_transposed, g - 1)
                for b in range(g * GROUP, (g + 1) * GROUP):
                    last = nc.gpsimd.tensor_scalar(xn[:, g % 2, b % GROUP, :], x_sb[:, b, :], rstd[:, b:b + 1],
                                                   neg_mean_rstd[:, b:b + 1], ALU.mult, ALU.add)
                last.then_inc(xn_ready, 1)

            pool.wait_ge(w_hi_ready, 1)
            nc.gpsimd.tensor_tensor(w_sa_lo[:, :, :], w_sa_sb[:, :, :], w_sa_hi[:, :, :].bitcast(f32),
                                    ALU.subtract).then_inc(w_lo_ready, 1)
            pool.wait_ge(w_hi_ready, 2)
            nc.gpsimd.tensor_tensor(w_cat_lo[:, :, :], w_cat[:, :, :], w_cat_hi[:, :, :].bitcast(f32),
                                    ALU.subtract).then_inc(w_lo_ready, 1)

            def clear(s, t):
                n = s * TILES + t
                used = apart(pool, n - ERING + 1)
                if later(s) or t >= ERING:
                    pool.wait_ge(e_lo_ready, used)
                nc.gpsimd.memset(e[:, t % ERING], 0.0).then_inc(e_zeroed, 1)

            def step(s, t):
                following = ahead_of(s, t, CLEAR_AHEAD)
                if not ended(*following):
                    clear(*following)
                pool.wait_ge(e_hi_ready, s * TILES + t + 1)
                nc.gpsimd.tensor_tensor(e_lo[:, t % RING], e[:, t % ERING], e_hi[:, t % RING].bitcast(f32),
                                        ALU.subtract).then_inc(e_lo_ready, 1)

            def finish(s):
                count = apart(pool, s + 1)
                pool.wait_ge(tanh_ready, count)
                nc.gpsimd.tensor_scalar(sig[:, :, :], sig[:, :, :], 0.5, 0.5, ALU.mult,
                                        ALU.add).then_inc(sig_ready, 1)
                pool.wait_ge(sig_ready, s + 1)
                if later(s):
                    pool.wait_ge(stored, 16 * s)
                nc.gpsimd.tensor_tensor(y[:, :, :], sig[:, :, :], x_sb[:, bass.ds(s * RB, RB), :],
                                        ALU.add).then_inc(y_ready, 1)

            normalise(2)
            normalise(3)
            for t in range(CLEAR_AHEAD):
                clear(0, t)
            for t in range(STORE):
                step(0, t)
            for at, t in body(0, STORE):
                step(at, t)
            finish(0)
            with pool.Fori(1, BLOCKS - 1) as s:
                for at, t in body(s, STORE):
                    step(at, t)
                finish(s)
            for t in range(STORE, TILES):
                step(BLOCKS - 1, t)
            finish(BLOCKS - 1)

        @block.scalar
        def _(act):
            act.dma_start(gate_rows[0:2, :], wa.rearrange("o (h d) -> (o h) d", h=2)).then_inc(rows_loaded, 16)
            act.dma_start(gate_rows[2:4, :], wb.rearrange("o (h d) -> (o h) d", h=2)).then_inc(rows_loaded, 16)
            act.wait_ge(ident_ready, 1)
            nc.scalar.activation(warm[:, :], ident[:, 0:1], ACT.Sqrt, bias=LN_EPS)
            act.dma_start(own_bias[:, 0:1], ba.unsqueeze(0).broadcast_to([P, 1])).then_inc(bias_loaded, 16)
            act.dma_start(own_bias[:, 1:2], bb.unsqueeze(0).broadcast_to([P, 1])).then_inc(bias_loaded, 16)
            act.dma_start(b_all[:, 0:D], b_gcnb.unsqueeze(0).broadcast_to([P, D])).then_inc(bias_loaded, 16)

            def standard_deviation(g):
                act.wait_ge(var_ready, g + 1)
                tokens = slice(g * GROUP, (g + 1) * GROUP)
                nc.scalar.activation(std[:, tokens], mean_var[:, tokens, 1], ACT.Sqrt,
                                     bias=LN_EPS).then_inc(std_ready, 1)

            def normalise(g):
                act.wait_ge(rstd_ready, g + 1)
                for b in range(g * GROUP, (g + 1) * GROUP):
                    last = nc.scalar.activation(xn[:, g % 2, b % GROUP, :], x_sb[:, b, :], ACT.Identity,
                                                bias=neg_mean_rstd[:, b:b + 1], scale=rstd[:, b:b + 1])
                last.then_inc(xn_ready, 1)

            def hidden_hi(g):
                act.wait_ge(xn_transposed, g + 1)
                if g >= 2:
                    act.wait_ge(unit_done, 2 * GROUP * (g - 1))
                for c in range(DC):
                    nc.scalar.activation(hnT_hi[:, g % 2, c, :], bank[4 + DC * (g % 2) + c][:, :],
                                         ACT.Relu).then_inc(hnT_hi_ready, 1)

            def products_hi(g, part):
                for j in range(g * GROUP + part * SPLIT, g * GROUP + (part + 1) * SPLIT):
                    u = 2 * j
                    act.wait_ge(unit_done, u + 1)
                    nc.scalar.activation(g_hi[:, j, :], bank[u % UNIT_BANKS][:, 0:SUM],
                                         ACT.Copy).then_inc(unit_hi_taken, 1)
                    u += 1
                    act.wait_ge(unit_done, u + 1)
                    nc.scalar.activation(h_hi[:, j, 0:D], bank[u % UNIT_BANKS][:, 0:D],
                                         ACT.Copy).then_inc(unit_hi_taken, 1)

            def take_sl(g):
                act.wait_ge(sl_spread, g + 1)
                tokens = slice(g * GW, (g + 1) * GW)
                nc.scalar.activation(neg_sl01[:, tokens], bank[3][:, :], ACT.Copy, scale=SLOPE)
                nc.scalar.activation(neg_sl[:, tokens], bank[3][:, :], ACT.Copy).then_inc(sl_taken, 1)

            def exponential(s, t):
                act.wait_ge(arg_ready, s * TILES + t + 1)
                for b in range(TB):
                    j = t * TB + b
                    last = nc.scalar.activation(score[:, t % RING, b, :], score[:, t % RING, b, :], ACT.Exp,
                                                bias=own[:, j, RIGHT01:RIGHT01 + 1])
                last.then_inc(exp_ready, 1)

            def take_adj(s, t):
                n = s * TILES + t
                act.wait_ge(tile_transposed, n + 1)
                if not isinstance(n, int) or n >= RING:
                    act.wait_ge(tile_summed, n - RING + 1)
                nc.scalar.activation(adjT[:, t % RING], staged[t % RING], ACT.Copy).then_inc(adjT_ready, 1)

            def step(s, t):
                following = ahead_of(s, t, 1)
                if not ended(*following):
                    exponential(*following)
                    take_adj(*following)
                act.wait_ge(e_ready, s * TILES + t + 1)
                nc.scalar.activation(e_hi[:, t % RING], e[:, t % ERING], ACT.Copy).then_inc(e_hi_ready, 1)

            def take_sums(s):
                if later(s):
                    act.wait_ge(att_ready, s)
                for r in range(RB):
                    wait_rows_summed(act, s, r)
                    nc.scalar.activation(att_sum[:, r, :], att_acc[r][:, 0:SUM],
                                         ACT.Copy).then_inc(att_sum_ready[r], 1)
                act.wait_ge(logit_ready, s + 1)
                nc.scalar.activation(exp_neg[:, :, :], logit[:, :, :], ACT.Exp, scale=-1.0).then_inc(exp_neg_ready, 1)

            def finish(s):
                act.wait_ge(mixed_ready, s + 1)
                if later(s):
                    act.wait_ge(y_ready, s)
                nc.scalar.activation(sig[:, :, :], mixed[:, :, :], ACT.Tanh, scale=0.5).then_inc(tanh_ready, 1)

            def run(tiles, s):
                for at, t in tiles:
                    if t == TAKE:
                        take_sums(s)
                    step(at, t)
                finish(s)

            standard_deviation(0)
            act.wait_ge(w_loaded, 16 * W_LOADS)
            nc.scalar.activation(w_sa_hi[:, :, :], w_sa_sb[:, :, :], ACT.Copy).then_inc(w_hi_ready, 1)
            normalise(0)
            act.wait_ge(w_cat_ready, 1)
            nc.scalar.activation(w_cat_hi[:, :, :], w_cat[:, :, :], ACT.Copy).then_inc(w_hi_ready, 1)
            standard_deviation(1)
            normalise(1)
            hidden_hi(0)
            standard_deviation(2)
            hidden_hi(1)
            products_hi(0, 0)
            standard_deviation(3)
            products_hi(0, 1)
            hidden_hi(2)
            products_hi(1, 0)
            take_sl(0)
            products_hi(1, 1)
            hidden_hi(3)
            products_hi(2, 0)
            take_sl(1)
            products_hi(2, 1)
            exponential(0, 0)
            take_adj(0, 0)
            products_hi(3, 0)
            take_sl(2)
            step(0, 0)
            products_hi(3, 1)
            take_sl(3)
            for t in range(1, MIX):
                step(0, t)
            run(body(0, MIX), 0)
            with act.Fori(1, BLOCKS - 1) as s:
                run(body(s, MIX), s)
            for t in range(MIX, TILES):
                step(BLOCKS - 1, t)
            take_sums(BLOCKS - 1)
            finish(BLOCKS - 1)

        @block.vector
        def _(dve):
            links = [0]

            def link(ins):
                links[0] += 1
                ins.then_inc(dve_steps, 1)
                dve.wait_ge(dve_steps, links[0])

            def statistics(g):
                blocks = range(g * GROUP, (g + 1) * GROUP)
                dve.wait_ge(x_loaded[g], 16)
                for b in blocks:
                    last = nc.vector.bn_stats(stats[:, b, :], x_sb[:, b, :])
                link(last)
                for b in blocks:
                    last = nc.vector.bn_aggr(mean_var[:, b, :], stats[:, b, :])
                last.then_inc(var_ready, 1)

            def inverse_deviation(g):
                blocks = slice(g * GROUP, (g + 1) * GROUP)
                dve.wait_ge(std_ready, g + 1)
                link(nc.vector.reciprocal(rstd[:, blocks], std[:, blocks]))
                nc.vector.scalar_tensor_tensor(neg_mean_rstd[:, blocks], mean_var[:, blocks, 0], -1.0, rstd[:, blocks],
                                               ALU.mult, ALU.mult).then_inc(rstd_ready, 1)

            def hidden_lo(g):
                for c in range(DC):
                    dve.wait_ge(hnT_hi_ready, g * DC + c + 1)
                    nc.vector.scalar_tensor_tensor(hnT_lo[:, g % 2, c, :], bank[4 + DC * (g % 2) + c][:, :], 0.0,
                                                   hnT_hi[:, g % 2, c, :].bitcast(f32), ALU.max,
                                                   ALU.subtract).then_inc(hnT_lo_ready, 1)

            def products_lo(g, part):
                for j in range(g * GROUP + part * SPLIT, g * GROUP + (part + 1) * SPLIT):
                    u = 2 * j
                    dve.wait_ge(unit_hi_taken, u + 1)
                    nc.vector.tensor_tensor(g_lo[:, j, :], bank[u % UNIT_BANKS][:, 0:SUM],
                                            g_hi[:, j, :].bitcast(f32), ALU.subtract)
                    nc.vector.tensor_tensor(own[:, j, :], bank[u % UNIT_BANKS][:, SELF:CAT], own_bias[:, :],
                                            ALU.add).then_inc(unit_lo_taken, 1)
                    u += 1
                    dve.wait_ge(unit_hi_taken, u + 1)
                    nc.vector.tensor_tensor(h_lo[:, j, :], bank[u % UNIT_BANKS][:, 0:D],
                                            h_hi[:, j, 0:D].bitcast(f32), ALU.subtract).then_inc(unit_lo_taken, 1)

            def argument(s, t):
                if later(s) or t >= RING:
                    dve.wait_ge(e_ready, s * TILES + t - RING + 1)
                rows = bass.ds(s * ROWS, ROWS)
                for b in range(TB):
                    j = t * TB + b
                    last = nc.vector.scalar_tensor_tensor(score[:, t % RING, b, :], neg_sl[:, rows],
                                                          own[:, j, RIGHT99:RIGHT99 + 1], neg_sl01[:, rows],
                                                          ALU.add, ALU.min)
                last.then_inc(arg_ready, 1)

            def step(s, t):
                n = s * TILES + t
                count = apart(dve, n + 1)
                dve.wait_ge(exp_ready, count)
                dve.wait_ge(e_zeroed, count)
                dve.wait_ge(adjT_ready, count)
                nc.vector.copy_predicated(e[:, t % ERING], staged[t % RING].bitcast(u16),
                                          score[:, t % RING]).then_inc(e_ready, 1)
                following = ahead_of(s, t, 2)
                if not ended(*following):
                    argument(*following)

            def take_sums(s):
                if later(s):
                    dve.wait_ge(mixed_ready, s)
                for r in range(RB):
                    wait_rows_summed(dve, s, r)
                    nc.vector.tensor_tensor(conv[:, r, :], adj_acc[r][:, 0:SUM], b_all[:, :],
                                            ALU.add).then_inc(conv_ready[r], 1)
                for r in range(RB):
                    dve.wait_ge(conv_ready[r], s + 1)
                nc.vector.tensor_tensor(logit[:, :, :], conv[:, :, GATE:GATE + 2],
                                        own[:, bass.ds(s * RB, RB), 0:2], ALU.add).then_inc(logit_ready, 1)

            def finish(s):
                for r in range(RB):
                    dve.wait_ge(att_sum_ready[r], s + 1)
                nc.vector.tensor_scalar(den[:, :], att_sum[:, :, D], DEN_EPS, None, ALU.add).then_inc(den_ready, 1)
                dve.wait_ge(exp_neg_ready, s + 1)
                nc.vector.tensor_scalar(one_plus[:, :, :], exp_neg[:, :, :], 1.0, None,
                                        ALU.add).then_inc(one_plus_ready, 1)
                dve.wait_ge(den_ready, s + 1)
                nc.vector.reciprocal(inv_den[:, :], den[:, :]).then_inc(inv_den_ready, 1)
                dve.wait_ge(one_plus_ready, s + 1)
                nc.vector.reciprocal(gate[:, :, :], one_plus[:, :, :]).then_inc(gate_ready, 1)
                dve.wait_ge(gate_ready, s + 1)
                dve.wait_ge(inv_den_ready, s + 1)
                nc.vector.tensor_tensor(att_scale[:, :], gate[:, :, 0], inv_den[:, :],
                                        ALU.mult).then_inc(att_scale_ready, 1)
                dve.wait_ge(att_scale_ready, s + 1)
                for r in range(RB):
                    last = nc.vector.tensor_scalar(att[:, r, :], att_sum[:, r, 0:D], att_scale[:, r:r + 1], None,
                                                   ALU.mult)
                last.then_inc(att_ready, 1)
                dve.wait_ge(att_ready, s + 1)
                if later(s):
                    dve.wait_ge(tanh_ready, s)
                for r in range(RB):
                    last = nc.vector.scalar_tensor_tensor(mixed[:, r, :], conv[:, r, 0:D], gate[:, r, 1:2],
                                                          att[:, r, :], ALU.mult, ALU.add)
                last.then_inc(mixed_ready, 1)

            def run(tiles, s):
                for at, t in tiles:
                    if t == TAKE:
                        take_sums(s)
                    step(at, t)
                finish(s)

            statistics(0)
            inverse_deviation(0)
            dve.wait_ge(w_loaded, 16 * W_LOADS)
            for c in range(DC):
                for k in range(2):
                    link(nc.vector.tensor_tensor_reduce(out=dot_junk[:, :], in0=w_sa_sb[:, c, :],
                                                        in1=a_all[:, k * D:(k + 1) * D], scale=-1.0, scalar=0.0,
                                                        op0=ALU.mult, op1=ALU.add,
                                                        accum_out=neg_v[:, c, k:k + 1]))
            for at, k, share in ((LEFT, 0, 1.0), (RIGHT99, 1, 1.0 - SLOPE), (RIGHT01, 1, SLOPE)):
                nc.vector.tensor_scalar(w_cat[:, :, SELF + at:SELF + at + 1], neg_v[:, :, k:k + 1], share, None,
                                        ALU.mult)
            dve.wait_ge(consts_ready, 1)
            dve.wait_ge(gate_cols_ready, 1)
            nc.vector.tensor_copy(w_cat[:, :, GATE:GATE + 4].rearrange("p c (h w) -> p c h w", h=2),
                                  bank[3][:, 0:4 * DC].rearrange("p (c w h) -> p c h w", c=DC, w=2)
                                  ).then_inc(w_cat_ready, 1)
            statistics(1)
            inverse_deviation(1)
            hidden_lo(0)
            statistics(2)
            inverse_deviation(2)
            hidden_lo(1)
            dve.wait_ge(bias_loaded, 16 * BIAS_LOADS)
            products_lo(0, 0)
            statistics(3)
            inverse_deviation(3)
            products_lo(0, 1)
            hidden_lo(2)
            products_lo(1, 0)
            products_lo(1, 1)
            hidden_lo(3)
            products_lo(2, 0)
            products_lo(2, 1)
            dve.wait_ge(sl_taken, 1)
            argument(0, 0)
            argument(0, 1)
            products_lo(3, 0)
            step(0, 0)
            products_lo(3, 1)
            dve.wait_ge(sl_taken, GROUPS)
            for t in range(1, MIX):
                step(0, t)
            run(body(0, MIX), 0)
            with dve.Fori(1, BLOCKS - 1) as s:
                run(body(s, MIX), s)
            for t in range(MIX, TILES):
                step(BLOCKS - 1, t)
            take_sums(BLOCKS - 1)
            finish(BLOCKS - 1)

        @block.tensor
        def _(pe):
            pe.wait_ge(ident_ready, 1)
            pe.wait_ge(rows_loaded, 32)
            for c in range(DC):
                last = nc.tensor.transpose(bank[3][:, 4 * c:4 * c + 4], gate_rows[0:4, c * P:(c + 1) * P],
                                           ident[0:4, 0:4])
            last.then_inc(gate_cols_ready, 1)

            def transpose_tokens(g):
                pe.wait_ge(xn_ready, g + 1)
                if g >= 2:
                    pe.wait_ge(hnT_hi_ready, DC * (g - 1))
                    pe.wait_ge(hnT_lo_ready, DC * (g - 1))
                for c in range(DC):
                    for b in range(GROUP):
                        last = nc.tensor.transpose(bank[4 + DC * (g % 2) + c][:, b * P:(b + 1) * P],
                                                   xn[:, g % 2, b, c * P:(c + 1) * P], ident[:, :])
                last.then_inc(xn_transposed, 1)

            def product(u, width, stationary, moving):
                if u >= UNIT_BANKS:
                    pe.wait_ge(unit_hi_taken, u - UNIT_BANKS + 1)
                    pe.wait_ge(unit_lo_taken, u - UNIT_BANKS + 1)
                (s_hi, s_lo), (m_hi, m_lo) = stationary, moving
                for c in range(DC):
                    for i, (lhs, rhs) in enumerate(((s_hi, m_hi), (s_hi, m_lo), (s_lo, m_hi))):
                        last = nc.tensor.matmul(bank[u % UNIT_BANKS][:, 0:width], lhs[:, c, :], rhs[:, c, :],
                                                start=c == 0 and i == 0, stop=c == DC - 1 and i == 2)
                last.then_inc(unit_done, 1)

            def products(g, part):
                pe.wait_ge(hnT_hi_ready, DC * (g + 1))
                pe.wait_ge(hnT_lo_ready, DC * (g + 1))
                for b in range(part * SPLIT, (part + 1) * SPLIT):
                    cols = slice(b * P, (b + 1) * P)
                    tokens = (hnT_hi[:, g % 2, :, cols], hnT_lo[:, g % 2, :, cols])
                    u = 2 * (g * GROUP + b)
                    product(u, CAT, tokens, (w_cat_hi, w_cat_lo))
                    product(u + 1, D, tokens, (w_sa_hi, w_sa_lo))

            def spread_sl(g):
                pe.wait_ge(unit_lo_taken, 2 * GROUP * (g + 1) - 1)
                if g:
                    pe.wait_ge(sl_taken, g)
                for b in range(GROUP):
                    j = g * GROUP + b
                    last = nc.tensor.transpose(bank[3][:, b * P:(b + 1) * P], own[:, j, LEFT:LEFT + 1].broadcast_to([P, P]),
                                               ident[:, :])
                last.then_inc(sl_spread, 1)

            def transpose_tile(s, t):
                n = s * TILES + t
                pe.wait_ge(adj_loaded[t // LOAD], 16 * (s + 1))
                if not isinstance(n, int) or n >= RING:
                    pe.wait_ge(e_ready, n - RING + 1)
                for b in range(TB):
                    for r in range(RB):
                        c0 = (t % LOAD) * TW + b * P
                        last = nc.tensor.transpose(staged[t % RING][:, b, r * P:(r + 1) * P],
                                                   adj_b[:, t // LOAD, r, c0:c0 + P], ident_b[:, :])
                last.then_inc(tile_transposed, 1)

            def sum_tile(s, t):
                n = s * TILES + t
                pe.wait_ge(adjT_ready, n + 1)
                pe.wait_ge(e_hi_ready, n + 1)
                pe.wait_ge(e_lo_ready, n + 1)
                for r in range(RB):
                    if t == 0 and later(s):
                        pe.wait_ge(conv_ready[r], s)
                        pe.wait_ge(att_sum_ready[r], s)
                    rows = slice(r * P, (r + 1) * P)
                    for b in range(TB):
                        j = t * TB + b
                        first, final = t == 0 and b == 0, t == TILES - 1 and b == TB - 1
                        a = adjT[:, t % RING, b, rows]
                        nc.tensor.matmul(adj_acc[r][:, 0:SUM], a, g_hi[:, j, :], start=first, stop=False)
                        nc.tensor.matmul(adj_acc[r][:, 0:SUM], a, g_lo[:, j, :], start=False, stop=final)
                        hi, lo = e_hi[:, t % RING, b, rows], e_lo[:, t % RING, b, rows]
                        nc.tensor.matmul(att_acc[r][:, 0:SUM], hi, h_hi[:, j, :], start=first, stop=False)
                        nc.tensor.matmul(att_acc[r][:, 0:D], hi, h_lo[:, j, :], start=False, stop=False)
                        last = nc.tensor.matmul(att_acc[r][:, 0:SUM], lo, h_hi[:, j, :], start=False, stop=final)
                    if t == TILES - 1 and r < RB - 1:
                        last.then_inc(rows_summed[r], 1)
                last.then_inc(tile_summed, 1)

            transpose_tokens(0)
            transpose_tokens(1)
            pe.wait_ge(w_lo_ready, 2)
            products(0, 0)
            products(0, 1)
            transpose_tokens(2)
            products(1, 0)
            spread_sl(0)
            products(1, 1)
            transpose_tokens(3)
            products(2, 0)
            spread_sl(1)
            products(2, 1)
            pe.wait_ge(hnT_lo_ready, DC * (GROUPS - 1))
            pe.wait_ge(ident_b_ready, 1)
            transpose_tile(0, 0)
            transpose_tile(0, 1)
            products(3, 0)
            spread_sl(2)
            transpose_tile(0, 2)
            transpose_tile(0, 3)
            products(3, 1)
            spread_sl(3)
            pe.wait_ge(consts_ready, 1)
            pe.wait_ge(unit_hi_taken, ALL_UNITS)
            pe.wait_ge(unit_lo_taken, ALL_UNITS)
            pe.wait_ge(sl_taken, GROUPS)

            def sum_block(s):
                for t in range(TILES):
                    following = ahead_of(s, t, STAGE_AHEAD)
                    if not ended(*following):
                        transpose_tile(*following)
                    sum_tile(s, t)

            sum_block(0)
            with pe.Fori(1, BLOCKS - 1) as s:
                sum_block(s)
            sum_block(BLOCKS - 1)



_INS = ['x', 'adj', 'L0_gnn_W_sa', 'L0_gnn_a_sa', 'L0_gnn_W_gcnb', 'L0_gnn_b_gcnb', 'L0_gnn_Wa', 'L0_gnn_ba',
        'L0_gnn_Wb', 'L0_gnn_bb']


def kernel(**inputs):
    import numpy as _np
    import concourse.bacc as _bacc
    from concourse import mybir as _mybir
    from concourse.bass_utils import run_bass_kernel_spmd as _run

    nc = _bacc.Bacc("TRN2", target_bir_lowering=False, num_devices=1)
    arrays, args = {}, []
    for name in _INS:
        a = _np.ascontiguousarray(inputs[name])
        arrays[f"in_{name}_dram"] = a
        args.append(nc.dram_tensor(f"in_{name}_dram", a.shape, _mybir.dt.from_np(a.dtype), kind="ExternalInput").ap())
    args.append(nc.dram_tensor("out_0_dram", inputs['x'].shape, _mybir.dt.float32, kind="ExternalOutput").ap())
    graph_layer(nc, *args)
    r = _run(nc, [arrays], core_ids=[0])
    return r.results[0]["out_0_dram"]
```

```python
import concourse.bass as bass
from concourse import mybir
from contextlib import ExitStack

P = 128


def graph_layer(nc, x, adj, w_sa, a_sa, w_gcnb, b_gcnb, wa, ba, wb, bb, out):
    f32, f32r = mybir.dt.float32, mybir.dt.float32r
    bf16, u16 = mybir.dt.bfloat16, mybir.dt.uint16
    ALU, ACT = mybir.AluOpType, mybir.ActivationFunctionType

    N, D = x.shape
    LN_EPS, DEN_EPS, SLOPE = 1e-5, 1e-5, 0.01
    DC = D // P
    JB = N // P
    GROUP = 4
    GROUPS = JB // GROUP
    GW = GROUP * P
    RB = 2
    ROWS = RB * P
    BLOCKS = N // ROWS
    TB = 2
    TW = TB * P
    TILES = N // TW
    LOAD = 2
    LOADS = TILES // LOAD
    SUM = D + 2
    GATE = D
    SELF = D + 2
    RIGHT99, RIGHT01, LEFT = 2, 3, 4
    OWN = 6
    CAT = SELF + OWN
    CLEAR_AHEAD = 2
    RING = 4
    ERING = 4
    STAGE_AHEAD = 4
    TAKE = 2
    WEIGH = 3
    BLEND = 4
    SQUASH = 5
    STORE = 6
    UNIT_BANKS = 3
    assert TILES % RING == 0 and TAKE < RING and STORE < TILES and N == BLOCKS * ROWS

    with ExitStack() as ctx:
        def sb(name, shape, dt=f32):
            return ctx.enter_context(nc.sbuf_tensor(name, [P] + shape, dt))

        def sem(name):
            return ctx.enter_context(nc.semaphore(name))

        BIAS_LOADS = 3
        ident = sb("ident", [P])
        ident_b = sb("ident_b", [P], bf16)
        x_sb = sb("x_sb", [JB, D])
        stats = sb("stats", [JB, 6])
        mean_var = sb("mean_var", [JB, 2])
        std = sb("std", [JB])
        rstd = sb("rstd", [JB])
        neg_mean_rstd = sb("neg_mean_rstd", [JB])
        warm = sb("warm", [1])
        xn = sb("xn", [2, GROUP, D])
        hnT_hi = sb("hnT_hi", [2, DC, GW], f32r)
        hnT_lo = sb("hnT_lo", [2, DC, GW], f32r)
        w_sa_sb = sb("w_sa_sb", [DC, D])
        w_sa_hi = sb("w_sa_hi", [DC, D], f32r)
        w_sa_lo = sb("w_sa_lo", [DC, D], f32r)
        w_cat = sb("w_cat", [DC, CAT])
        w_cat_hi = sb("w_cat_hi", [DC, CAT], f32r)
        w_cat_lo = sb("w_cat_lo", [DC, CAT], f32r)
        gate_rows = sb("gate_rows", [D])
        a_all = sb("a_all", [2 * D])
        b_all = sb("b_all", [SUM])
        own_bias = sb("own_bias", [OWN])
        dot_junk = sb("dot_junk", [D])
        neg_v = sb("neg_v", [DC, 2])
        neg_sl = sb("neg_sl", [N])
        neg_sl01 = sb("neg_sl01", [N])
        own = sb("own", [JB, OWN])
        g_hi = sb("g_hi", [JB, SUM], f32r)
        g_lo = sb("g_lo", [JB, SUM], f32r)
        h_hi = sb("h_hi", [JB, SUM], f32r)
        h_lo = sb("h_lo", [JB, D], f32r)

        adj_sb = sb("adj_sb", [LOADS, RB, LOAD * TW])
        score = sb("score", [RING, TB, ROWS])
        e = sb("e", [ERING, TB, ROWS])
        adjT = sb("adjT", [RING, TB, ROWS], f32r)
        e_hi = sb("e_hi", [RING, TB, ROWS], f32r)
        e_lo = sb("e_lo", [RING, TB, ROWS], f32r)

        conv = sb("conv", [RB, SUM])
        att_sum = sb("att_sum", [RB, SUM])
        logit = sb("logit", [RB, 2])
        exp_neg = sb("exp_neg", [RB, 2])
        one_plus = sb("one_plus", [RB, 2])
        gate = sb("gate", [RB, 2])
        den = sb("den", [RB])
        inv_den = sb("inv_den", [RB])
        att_scale = sb("att_scale", [RB])
        att = sb("att", [RB, D])
        mixed = sb("mixed", [RB, D])
        sig = sb("sig", [RB, D])
        y = sb("y", [RB, D])

        bank = [ctx.enter_context(nc.psum_tensor(f"bank{i}", [P, 512], f32)) for i in range(8)]
        adj_acc, att_acc = bank[0:RB], bank[RB:2 * RB]
        staged = [bank[4 + i][:, :].bitcast(bf16)[:, 0:TB * ROWS].rearrange("p (b r) -> p b r", b=TB)
                  for i in range(RING)]
        adj_b = adj_sb[:, :, :, :].bitcast(bf16).rearrange("p q r (j two) -> p q r j two", two=2)[:, :, :, :, 1]

        x_loaded = [sem(f"x_loaded{g}") for g in range(GROUPS)]
        w_sa_loaded = sem("w_sa_loaded")
        a_loaded = sem("a_loaded")
        w_gcnb_loaded = sem("w_gcnb_loaded")
        bias_loaded = sem("bias_loaded")
        rows_loaded = sem("rows_loaded")
        adj_loaded = [sem(f"adj_loaded{q}") for q in range(LOADS)]
        ident_cleared = sem("ident_cleared")
        ident_ready = sem("ident_ready")
        ident_b_ready = sem("ident_b_ready")
        consts_ready = sem("consts_ready")
        dve_steps = sem("dve_steps")
        stats_ready = sem("stats_ready")
        var_ready = sem("var_ready")
        std_ready = sem("std_ready")
        rstd_ready = sem("rstd_ready")
        xn_ready = [sem(f"xn_ready{h}") for h in range(2)]
        gate_cols_ready = sem("gate_cols_ready")
        w_cat_ready = sem("w_cat_ready")
        w_sa_hi_ready = sem("w_sa_hi_ready")
        w_cat_hi_ready = sem("w_cat_hi_ready")
        w_lo_ready = sem("w_lo_ready")
        xn_transposed = sem("xn_transposed")
        hnT_hi_ready = sem("hnT_hi_ready")
        hnT_lo_ready = sem("hnT_lo_ready")
        unit_done = sem("unit_done")
        unit_hi_taken = sem("unit_hi_taken")
        unit_lo_taken = sem("unit_lo_taken")
        sl_spread = sem("sl_spread")
        sl_taken = sem("sl_taken")
        sl01_ready = sem("sl01_ready")

        arg_ready = sem("arg_ready")
        exp_ready = sem("exp_ready")
        e_zeroed = sem("e_zeroed")
        tile_transposed = sem("tile_transposed")
        adjT_ready = sem("adjT_ready")
        e_ready = sem("e_ready")
        e_hi_ready = sem("e_hi_ready")
        e_lo_ready = sem("e_lo_ready")
        tile_summed = sem("tile_summed")
        rows_summed = [sem(f"rows_summed{r}") for r in range(RB - 1)]
        conv_ready = [sem(f"conv_ready{r}") for r in range(RB)]
        att_sum_ready = [sem(f"att_sum_ready{r}") for r in range(RB)]
        logit_ready = sem("logit_ready")
        exp_neg_ready = sem("exp_neg_ready")
        den_ready = sem("den_ready")
        inv_den_ready = sem("inv_den_ready")
        one_plus_ready = sem("one_plus_ready")
        gate_ready = sem("gate_ready")
        att_scale_ready = sem("att_scale_ready")
        att_ready = sem("att_ready")
        mixed_ready = sem("mixed_ready")
        tanh_ready = sem("tanh_ready")
        sig_ready = sem("sig_ready")
        y_ready = sem("y_ready")
        shifted = sem("shifted")
        last_y_ready = [sem(f"last_y_ready{r}") for r in range(RB)]
        stored = sem("stored")

        ALL_UNITS = 2 * JB
        ALL_ROWS = slice(0, RB)

        def later(s):
            return not isinstance(s, int) or s > 0

        def apart(engine, value):
            value = value if isinstance(value, int) else engine.to_reg(value)
            engine.wait_ge(ident_ready, 1)
            return value

        def body(s, ahead):
            return [(s, t) for t in range(ahead, TILES)] + [(s + 1, t) for t in range(ahead)]

        def ahead_of(s, t, k):
            return (s, t + k) if t + k < TILES else (s + 1, t + k - TILES)

        def halves(g):
            return [range(g * GROUP + h * GROUP // 2, g * GROUP + (h + 1) * GROUP // 2) for h in range(2)]

        def ended(s, t):
            return isinstance(s, int) and s >= BLOCKS

        def wait_rows_summed(engine, s, r):
            if r < RB - 1:
                engine.wait_ge(rows_summed[r], s + 1)
            else:
                engine.wait_ge(tile_summed, TILES * (s + 1))

        x_rows = x.rearrange("(g b p) d -> g p b d", p=P, b=GROUP)
        adj_rows = adj.rearrange("(s r p) j -> s p r j", p=P, r=RB)
        out_rows = out.rearrange("(s r p) d -> s p r d", p=P, r=RB)

        block = ctx.enter_context(nc.Block())

        @block.sync
        def _(sp):
            def load_x(g):
                sp.dma_start(x_sb[:, g * GROUP:(g + 1) * GROUP, :], x_rows[g]).then_inc(x_loaded[g], 16)

            load_x(0)
            sp.dma_start(w_sa_sb[:, :, :], w_sa.rearrange("(c p) n -> p c n", p=P)).then_inc(w_sa_loaded, 16)
            sp.dma_start(a_all[:, :], a_sa.broadcast_to([P, 2 * D])).then_inc(a_loaded, 16)
            sp.dma_start(w_cat[:, :, 0:D], w_gcnb.rearrange("(c p) n -> p c n", p=P)).then_inc(w_gcnb_loaded, 16)
            for g in range(1, GROUPS):
                load_x(g)

            def load(s, q):
                cols = slice(q * LOAD * TW, (q + 1) * LOAD * TW)
                sp.dma_start(adj_sb[:, q, :, :], adj_rows[s, :, :, cols]).then_inc(adj_loaded[q], 16)

            def store(s):
                sp.wait_ge(y_ready, s + 1)
                sp.dma_start(out_rows[s], y[:, :, :]).then_inc(stored, 16)

            def load_block(s):
                for q in range(LOADS):
                    sp.wait_ge(tile_transposed, TILES * (s - 1) + LOAD * (q + 1))
                    load(s, q)

            for q in range(LOADS):
                load(0, q)
            load_block(1)
            with sp.Fori(2, BLOCKS) as s:
                load_block(s)
                store(s - 2)
            store(BLOCKS - 2)
            for r in range(RB):
                sp.wait_ge(last_y_ready[r], 1)
                sp.dma_start(out_rows[BLOCKS - 1][:, r, :], y[:, r, :]).then_inc(stored, 16)
            sp.wait_ge(stored, 16 * (BLOCKS - 1 + RB))

        @block.gpsimd
        def _(pool):
            nc.gpsimd.memset(ident[:, :], 0.0).then_inc(ident_cleared, 1)
            pool.wait_ge(ident_cleared, 1)
            nc.gpsimd.affine_select(out=ident[:, :], in_=ident[:, :], compare_op=ALU.not_equal, fill=1.0,
                                    base=0, pattern=[[-1, P]], channel_multiplier=1).then_inc(ident_ready, 1)
            nc.gpsimd.memset(h_hi[:, :, D:D + 1].bitcast(f32), 1.0)
            nc.gpsimd.memset(h_hi[:, :, D + 1:SUM].bitcast(f32), 0.0)
            nc.gpsimd.memset(b_all[:, D:SUM], 0.0)
            nc.gpsimd.memset(w_cat[:, :, CAT - 1:CAT], 0.0)
            nc.gpsimd.memset(own_bias[:, 2:OWN], 0.0).then_inc(consts_ready, 1)
            pool.wait_ge(ident_ready, 1)
            nc.gpsimd.tensor_copy(ident_b[:, :], ident[:, :]).then_inc(ident_b_ready, 1)

            def normalise(g, half):
                pool.wait_ge(rstd_ready, g + 1)
                if g >= 2:
                    pool.wait_ge(xn_transposed, g - 1)
                for b in halves(g)[half]:
                    last = nc.gpsimd.tensor_scalar(xn[:, g % 2, b % GROUP, :], x_sb[:, b, :], rstd[:, b:b + 1],
                                                   neg_mean_rstd[:, b:b + 1], ALU.mult, ALU.add)
                last.then_inc(xn_ready[half], 1)

            def scale_sl(g):
                pool.wait_ge(sl_taken, g + 1)
                tokens = slice(g * GW, (g + 1) * GW)
                nc.gpsimd.tensor_scalar(neg_sl01[:, tokens], neg_sl[:, tokens], SLOPE, None,
                                        ALU.mult).then_inc(sl01_ready, 1)

            def clear(s, t):
                n = s * TILES + t
                used = apart(pool, n - ERING + 1)
                if later(s) or t >= ERING:
                    pool.wait_ge(e_lo_ready, used)
                nc.gpsimd.memset(e[:, t % ERING], 0.0).then_inc(e_zeroed, 1)

            def step(s, t):
                following = ahead_of(s, t, CLEAR_AHEAD)
                if not ended(*following):
                    clear(*following)
                pool.wait_ge(e_hi_ready, s * TILES + t + 1)
                nc.gpsimd.tensor_tensor(e_lo[:, t % RING], e[:, t % ERING], e_hi[:, t % RING].bitcast(f32),
                                        ALU.subtract).then_inc(e_lo_ready, 1)

            def finish(s):
                count = apart(pool, s + 1)
                pool.wait_ge(tanh_ready, count)
                nc.gpsimd.tensor_scalar(sig[:, :, :], sig[:, :, :], 0.5, 0.5, ALU.mult,
                                        ALU.add).then_inc(sig_ready, 1)
                pool.wait_ge(sig_ready, s + 1)
                if later(s):
                    pool.wait_ge(stored, 16 * s)
                nc.gpsimd.tensor_tensor(y[:, :, :], sig[:, :, :], x_sb[:, bass.ds(s * RB, RB), :],
                                        ALU.add).then_inc(y_ready, 1)

            pool.wait_ge(w_sa_hi_ready, 1)
            nc.gpsimd.tensor_tensor(w_sa_lo[:, :, :], w_sa_sb[:, :, :], w_sa_hi[:, :, :].bitcast(f32),
                                    ALU.subtract).then_inc(w_lo_ready, 1)
            normalise(0, 1)
            pool.wait_ge(w_cat_hi_ready, 1)
            nc.gpsimd.tensor_tensor(w_cat_lo[:, :, :], w_cat[:, :, :], w_cat_hi[:, :, :].bitcast(f32),
                                    ALU.subtract).then_inc(w_lo_ready, 1)
            normalise(1, 1)
            for t in range(CLEAR_AHEAD):
                clear(0, t)
            for g in range(2, GROUPS):
                for half in range(2):
                    normalise(g, half)
                scale_sl(g - 2)
            step(0, 0)
            scale_sl(GROUPS - 2)
            step(0, 1)
            scale_sl(GROUPS - 1)
            for t in range(2, STORE + 1):
                step(0, t)
            for at, t in body(0, STORE + 1):
                step(at, t)
            finish(0)
            with pool.Fori(1, BLOCKS - 1) as s:
                for at, t in body(s, STORE + 1):
                    step(at, t)
                finish(s)
            for t in range(STORE + 1, TILES):
                step(BLOCKS - 1, t)
            nc.gpsimd.tensor_scalar(x_sb[:, JB - RB:JB, :], x_sb[:, JB - RB:JB, :], 0.5, None,
                                    ALU.add).then_inc(shifted, 1)

        @block.scalar
        def _(act):
            act.dma_start(gate_rows[0:2, :], wa.rearrange("o (h d) -> (o h) d", h=2)).then_inc(rows_loaded, 16)
            act.dma_start(gate_rows[2:4, :], wb.rearrange("o (h d) -> (o h) d", h=2)).then_inc(rows_loaded, 16)
            act.wait_ge(ident_ready, 1)
            nc.scalar.activation(warm[:, :], ident[:, 0:1], ACT.Sqrt, bias=LN_EPS)
            act.dma_start(own_bias[:, 0:1], ba.unsqueeze(0).broadcast_to([P, 1])).then_inc(bias_loaded, 16)
            act.dma_start(own_bias[:, 1:2], bb.unsqueeze(0).broadcast_to([P, 1])).then_inc(bias_loaded, 16)
            act.dma_start(b_all[:, 0:D], b_gcnb.unsqueeze(0).broadcast_to([P, D])).then_inc(bias_loaded, 16)

            def standard_deviation(g):
                act.wait_ge(var_ready, g + 1)
                tokens = slice(g * GROUP, (g + 1) * GROUP)
                nc.scalar.activation(std[:, tokens], mean_var[:, tokens, 1], ACT.Sqrt,
                                     bias=LN_EPS).then_inc(std_ready, 1)

            def normalise(g):
                act.wait_ge(rstd_ready, g + 1)
                for b in halves(g)[0]:
                    last = nc.scalar.activation(xn[:, g % 2, b % GROUP, :], x_sb[:, b, :], ACT.Identity,
                                                bias=neg_mean_rstd[:, b:b + 1], scale=rstd[:, b:b + 1])
                last.then_inc(xn_ready[0], 1)

            def hidden_hi(g):
                act.wait_ge(xn_transposed, g + 1)
                if g >= 2:
                    act.wait_ge(unit_done, 2 * GROUP * (g - 1))
                for c in range(DC):
                    nc.scalar.activation(hnT_hi[:, g % 2, c, :], bank[4 + DC * (g % 2) + c][:, :],
                                         ACT.Relu).then_inc(hnT_hi_ready, 1)

            def products_hi(*blocks):
                for j in blocks:
                    u = 2 * j
                    act.wait_ge(unit_done, u + 1)
                    nc.scalar.activation(g_hi[:, j, :], bank[u % UNIT_BANKS][:, 0:SUM],
                                         ACT.Copy).then_inc(unit_hi_taken, 1)
                    u += 1
                    act.wait_ge(unit_done, u + 1)
                    nc.scalar.activation(h_hi[:, j, 0:D], bank[u % UNIT_BANKS][:, 0:D],
                                         ACT.Copy).then_inc(unit_hi_taken, 1)

            def take_sl(g):
                act.wait_ge(sl_spread, g + 1)
                nc.scalar.activation(neg_sl[:, g * GW:(g + 1) * GW], bank[3][:, :], ACT.Copy).then_inc(sl_taken, 1)

            def exponential(s, t):
                act.wait_ge(arg_ready, s * TILES + t + 1)
                for b in range(TB):
                    j = t * TB + b
                    last = nc.scalar.activation(score[:, t % RING, b, :], score[:, t % RING, b, :], ACT.Exp,
                                                bias=own[:, j, RIGHT01:RIGHT01 + 1])
                last.then_inc(exp_ready, 1)

            def take_adj(s, t):
                n = s * TILES + t
                act.wait_ge(tile_transposed, n + 1)
                if not isinstance(n, int) or n >= RING:
                    act.wait_ge(tile_summed, n - RING + 1)
                nc.scalar.activation(adjT[:, t % RING], staged[t % RING], ACT.Copy).then_inc(adjT_ready, 1)

            def high_part(s, t):
                act.wait_ge(e_ready, s * TILES + t + 1)
                nc.scalar.activation(e_hi[:, t % RING], e[:, t % ERING], ACT.Copy).then_inc(e_hi_ready, 1)

            def step(s, t):
                following = ahead_of(s, t, 1)
                if not ended(*following):
                    exponential(*following)
                    take_adj(*following)
                high_part(s, t)

            def take_sums(s, blocks=range(RB)):
                if later(s):
                    act.wait_ge(att_ready, s)
                for r in blocks:
                    wait_rows_summed(act, s, r)
                    nc.scalar.activation(att_sum[:, r, :], att_acc[r][:, 0:SUM],
                                         ACT.Copy).then_inc(att_sum_ready[r], 1)

            def gate_exponential(s, rows=ALL_ROWS, part=0):
                act.wait_ge(logit_ready, s + part + 1)
                nc.scalar.activation(exp_neg[:, rows, :], logit[:, rows, :], ACT.Exp,
                                     scale=-1.0).then_inc(exp_neg_ready, 1)

            def squash(s, rows=ALL_ROWS, part=0):
                act.wait_ge(mixed_ready, s + part + 1)
                if later(s):
                    act.wait_ge(y_ready, s)
                nc.scalar.activation(sig[:, rows, :], mixed[:, rows, :], ACT.Tanh, scale=0.5).then_inc(tanh_ready, 1)

            def run(s):
                for at, t in body(s, SQUASH + 1):
                    if t == TAKE:
                        exponential(at, t + 1)
                        high_part(at, t)
                        take_sums(s)
                        take_adj(at, t + 1)
                        gate_exponential(s)
                    else:
                        step(at, t)
                squash(s)

            act.wait_ge(w_sa_loaded, 16)
            nc.scalar.activation(w_sa_hi[:, :, :], w_sa_sb[:, :, :], ACT.Copy).then_inc(w_sa_hi_ready, 1)
            standard_deviation(0)
            normalise(0)
            act.wait_ge(w_cat_ready, 1)
            nc.scalar.activation(w_cat_hi[:, :, :], w_cat[:, :, :], ACT.Copy).then_inc(w_cat_hi_ready, 1)
            hidden_hi(0)
            standard_deviation(1)
            normalise(1)
            products_hi(0, 1)
            hidden_hi(1)
            products_hi(2, 3, 4)
            standard_deviation(2)
            products_hi(5)
            take_sl(0)
            products_hi(6)
            hidden_hi(2)
            products_hi(7, 8)
            standard_deviation(3)
            nc.scalar.activation(warm[:, :], ident[:, 0:1], ACT.Exp)
            products_hi(9)
            take_sl(1)
            exponential(0, 0)
            products_hi(10)
            hidden_hi(3)
            products_hi(11)
            take_adj(0, 0)
            exponential(0, 1)
            products_hi(12)
            take_adj(0, 1)
            products_hi(13)
            take_sl(2)
            high_part(0, 0)
            products_hi(14)
            exponential(0, 2)
            products_hi(15)
            take_sl(3)
            take_adj(0, 2)
            high_part(0, 1)
            for t in range(2, SQUASH + 1):
                step(0, t)
            run(0)
            with act.Fori(1, BLOCKS - 1) as s:
                run(s)
            for t in range(SQUASH + 1, TILES):
                step(BLOCKS - 1, t)
            for r in range(RB):
                take_sums(BLOCKS - 1, [r])
                gate_exponential(BLOCKS - 1, slice(r, r + 1), r)
            for r in range(RB):
                squash(BLOCKS - 1, slice(r, r + 1), r)

        @block.vector
        def _(dve):
            links = [0]

            def link(ins):
                links[0] += 1
                ins.then_inc(dve_steps, 1)
                dve.wait_ge(dve_steps, links[0])

            def measure(b):
                dve.wait_ge(x_loaded[b // GROUP], 16)
                nc.vector.bn_stats(stats[:, b, :], x_sb[:, b, :]).then_inc(stats_ready, 1)

            def variance(g):
                dve.wait_ge(stats_ready, (g + 1) * GROUP)
                for b in range(g * GROUP, (g + 1) * GROUP):
                    last = nc.vector.bn_aggr(mean_var[:, b, :], stats[:, b, :])
                last.then_inc(var_ready, 1)

            def inverse_deviation(g):
                blocks = slice(g * GROUP, (g + 1) * GROUP)
                dve.wait_ge(std_ready, g + 1)
                link(nc.vector.reciprocal(rstd[:, blocks], std[:, blocks]))
                nc.vector.scalar_tensor_tensor(neg_mean_rstd[:, blocks], mean_var[:, blocks, 0], -1.0, rstd[:, blocks],
                                               ALU.mult, ALU.mult).then_inc(rstd_ready, 1)

            def hidden_lo(g):
                for c in range(DC):
                    dve.wait_ge(hnT_hi_ready, g * DC + c + 1)
                    nc.vector.scalar_tensor_tensor(hnT_lo[:, g % 2, c, :], bank[4 + DC * (g % 2) + c][:, :], 0.0,
                                                   hnT_hi[:, g % 2, c, :].bitcast(f32), ALU.max,
                                                   ALU.subtract).then_inc(hnT_lo_ready, 1)

            def products_lo(*blocks):
                for j in blocks:
                    u = 2 * j
                    dve.wait_ge(unit_hi_taken, u + 1)
                    nc.vector.tensor_tensor(g_lo[:, j, :], bank[u % UNIT_BANKS][:, 0:SUM],
                                            g_hi[:, j, :].bitcast(f32), ALU.subtract)
                    nc.vector.tensor_tensor(own[:, j, :], bank[u % UNIT_BANKS][:, SELF:CAT], own_bias[:, :],
                                            ALU.add).then_inc(unit_lo_taken, 1)
                    u += 1
                    dve.wait_ge(unit_hi_taken, u + 1)
                    nc.vector.tensor_tensor(h_lo[:, j, :], bank[u % UNIT_BANKS][:, 0:D],
                                            h_hi[:, j, 0:D].bitcast(f32), ALU.subtract).then_inc(unit_lo_taken, 1)

            def argument(s, t):
                if later(s) or t >= RING:
                    dve.wait_ge(e_ready, s * TILES + t - RING + 1)
                rows = bass.ds(s * ROWS, ROWS)
                for b in range(TB):
                    j = t * TB + b
                    last = nc.vector.scalar_tensor_tensor(score[:, t % RING, b, :], neg_sl[:, rows],
                                                          own[:, j, RIGHT99:RIGHT99 + 1], neg_sl01[:, rows],
                                                          ALU.add, ALU.min)
                last.then_inc(arg_ready, 1)

            def select(s, t):
                n = s * TILES + t
                count = apart(dve, n + 1)
                dve.wait_ge(exp_ready, count)
                dve.wait_ge(e_zeroed, count)
                dve.wait_ge(adjT_ready, count)
                nc.vector.copy_predicated(e[:, t % ERING], staged[t % RING].bitcast(u16),
                                          score[:, t % RING]).then_inc(e_ready, 1)

            def step(s, t):
                select(s, t)
                following = ahead_of(s, t, 2)
                if not ended(*following):
                    argument(*following)

            def take_sums(s, rows=ALL_ROWS, part=0):
                blocks = range(rows.start, rows.stop)
                if later(s):
                    dve.wait_ge(mixed_ready, s)
                for r in blocks:
                    wait_rows_summed(dve, s, r)
                    nc.vector.tensor_tensor(conv[:, r, :], adj_acc[r][:, 0:SUM], b_all[:, :],
                                            ALU.add).then_inc(conv_ready[r], 1)
                for r in blocks:
                    dve.wait_ge(conv_ready[r], s + 1)
                nc.vector.tensor_tensor(logit[:, rows, :], conv[:, rows, GATE:GATE + 2],
                                        own[:, bass.ds(s * RB + rows.start, len(blocks)), 0:2],
                                        ALU.add).then_inc(logit_ready, 1)

            def weigh(s, rows=ALL_ROWS, part=0):
                count = s + part + 1
                for r in range(rows.start, rows.stop):
                    dve.wait_ge(att_sum_ready[r], s + 1)
                nc.vector.tensor_scalar(den[:, rows], att_sum[:, rows, D], DEN_EPS, None,
                                        ALU.add).then_inc(den_ready, 1)
                dve.wait_ge(exp_neg_ready, count)
                nc.vector.tensor_scalar(one_plus[:, rows, :], exp_neg[:, rows, :], 1.0, None,
                                        ALU.add).then_inc(one_plus_ready, 1)
                dve.wait_ge(den_ready, count)
                nc.vector.reciprocal(inv_den[:, rows], den[:, rows]).then_inc(inv_den_ready, 1)
                dve.wait_ge(one_plus_ready, count)
                nc.vector.reciprocal(gate[:, rows, :], one_plus[:, rows, :]).then_inc(gate_ready, 1)
                dve.wait_ge(gate_ready, count)
                dve.wait_ge(inv_den_ready, count)
                nc.vector.tensor_tensor(att_scale[:, rows], gate[:, rows, 0], inv_den[:, rows],
                                        ALU.mult).then_inc(att_scale_ready, 1)

            def blend(s, rows=ALL_ROWS, part=0):
                blocks = range(rows.start, rows.stop)
                dve.wait_ge(att_scale_ready, s + part + 1)
                for r in blocks:
                    last = nc.vector.tensor_scalar(att[:, r, :], att_sum[:, r, 0:D], att_scale[:, r:r + 1], None,
                                                   ALU.mult)
                last.then_inc(att_ready, 1)
                dve.wait_ge(att_ready, s + part + 1)
                if later(s):
                    dve.wait_ge(tanh_ready, s)
                for r in blocks:
                    last = nc.vector.scalar_tensor_tensor(mixed[:, r, :], conv[:, r, 0:D], gate[:, r, 1:2],
                                                          att[:, r, :], ALU.mult, ALU.add)
                last.then_inc(mixed_ready, 1)

            def run(s):
                for at, t in body(s, BLEND + 1):
                    step(at, t)
                    if t == TAKE:
                        take_sums(s)
                    elif t == WEIGH:
                        weigh(s)
                blend(s)

            for b in range(GROUP):
                measure(b)
            variance(0)
            inverse_deviation(0)
            dve.wait_ge(w_sa_loaded, 16)
            dve.wait_ge(a_loaded, 16)
            for c in range(DC):
                for k in range(2):
                    link(nc.vector.tensor_tensor_reduce(out=dot_junk[:, :], in0=w_sa_sb[:, c, :],
                                                        in1=a_all[:, k * D:(k + 1) * D], scale=-1.0, scalar=0.0,
                                                        op0=ALU.mult, op1=ALU.add,
                                                        accum_out=neg_v[:, c, k:k + 1]))
            for at, k, share in ((LEFT, 0, 1.0), (RIGHT99, 1, 1.0 - SLOPE), (RIGHT01, 1, SLOPE)):
                nc.vector.tensor_scalar(w_cat[:, :, SELF + at:SELF + at + 1], neg_v[:, :, k:k + 1], share, None,
                                        ALU.mult)
            dve.wait_ge(w_gcnb_loaded, 16)
            dve.wait_ge(consts_ready, 1)
            dve.wait_ge(gate_cols_ready, 1)
            nc.vector.tensor_copy(w_cat[:, :, GATE:GATE + 4].rearrange("p c (h w) -> p c h w", h=2),
                                  bank[3][:, 0:4 * DC].rearrange("p (c w h) -> p c h w", c=DC, w=2)
                                  ).then_inc(w_cat_ready, 1)
            hidden_lo(0)
            for b in range(GROUP, 2 * GROUP):
                measure(b)
            variance(1)
            inverse_deviation(1)
            dve.wait_ge(bias_loaded, 16 * BIAS_LOADS)
            products_lo(0)
            measure(8)
            products_lo(1)
            measure(9)
            hidden_lo(1)
            products_lo(2)
            measure(10)
            products_lo(3)
            measure(11)
            variance(2)
            products_lo(4)
            inverse_deviation(2)
            products_lo(5)
            measure(12)
            measure(13)
            products_lo(6)
            hidden_lo(2)
            products_lo(7)
            measure(14)
            measure(15)
            variance(3)
            products_lo(8)
            inverse_deviation(3)
            dve.wait_ge(sl01_ready, 1)
            argument(0, 0)
            products_lo(9)
            argument(0, 1)
            products_lo(10)
            hidden_lo(3)
            products_lo(11)
            argument(0, 2)
            products_lo(12)
            select(0, 0)
            products_lo(13)
            argument(0, 3)
            products_lo(14)
            select(0, 1)
            products_lo(15)
            for t in range(2, BLEND + 1):
                step(0, t)
            run(0)
            dve.wait_ge(sl01_ready, GROUPS)
            with dve.Fori(1, BLOCKS - 1) as s:
                run(s)
            for t in range(BLEND + 1, TILES):
                step(BLOCKS - 1, t)
            parts = [(slice(r, r + 1), r) for r in range(RB)]
            for rows, r in parts:
                take_sums(BLOCKS - 1, rows, r)
            for rows, r in parts:
                weigh(BLOCKS - 1, rows, r)
                blend(BLOCKS - 1, rows, r)
            dve.wait_ge(shifted, 1)
            dve.wait_ge(stored, 16 * (BLOCKS - 1))
            for rows, r in parts:
                dve.wait_ge(tanh_ready, BLOCKS + r)
                nc.vector.scalar_tensor_tensor(y[:, r, :], sig[:, r, :], 0.5, x_sb[:, JB - RB + r, :],
                                               ALU.mult, ALU.add).then_inc(last_y_ready[r], 1)

        @block.tensor
        def _(pe):
            pe.wait_ge(ident_ready, 1)
            pe.wait_ge(rows_loaded, 32)
            for c in range(DC):
                last = nc.tensor.transpose(bank[3][:, 4 * c:4 * c + 4], gate_rows[0:4, c * P:(c + 1) * P],
                                           ident[0:4, 0:4])
            last.then_inc(gate_cols_ready, 1)

            def transpose_tokens(g):
                for half in range(2):
                    pe.wait_ge(xn_ready[half], g + 1)
                if g >= 2:
                    pe.wait_ge(hnT_hi_ready, DC * (g - 1))
                    pe.wait_ge(hnT_lo_ready, DC * (g - 1))
                for c in range(DC):
                    for b in range(GROUP):
                        last = nc.tensor.transpose(bank[4 + DC * (g % 2) + c][:, b * P:(b + 1) * P],
                                                   xn[:, g % 2, b, c * P:(c + 1) * P], ident[:, :])
                last.then_inc(xn_transposed, 1)

            def product(u, width, stationary, moving):
                if u >= UNIT_BANKS:
                    pe.wait_ge(unit_hi_taken, u - UNIT_BANKS + 1)
                    pe.wait_ge(unit_lo_taken, u - UNIT_BANKS + 1)
                (s_hi, s_lo), (m_hi, m_lo) = stationary, moving
                for c in range(DC):
                    for i, (lhs, rhs) in enumerate(((s_hi, m_hi), (s_hi, m_lo), (s_lo, m_hi))):
                        last = nc.tensor.matmul(bank[u % UNIT_BANKS][:, 0:width], lhs[:, c, :], rhs[:, c, :],
                                                start=c == 0 and i == 0, stop=c == DC - 1 and i == 2)
                last.then_inc(unit_done, 1)

            def products(*blocks):
                for j in blocks:
                    g, b = j // GROUP, j % GROUP
                    if b == 0:
                        pe.wait_ge(hnT_hi_ready, DC * (g + 1))
                        pe.wait_ge(hnT_lo_ready, DC * (g + 1))
                    cols = slice(b * P, (b + 1) * P)
                    tokens = (hnT_hi[:, g % 2, :, cols], hnT_lo[:, g % 2, :, cols])
                    product(2 * j, CAT, tokens, (w_cat_hi, w_cat_lo))
                    product(2 * j + 1, D, tokens, (w_sa_hi, w_sa_lo))

            def spread_sl(g):
                pe.wait_ge(unit_lo_taken, 2 * GROUP * (g + 1) - 1)
                if g:
                    pe.wait_ge(sl_taken, g)
                for b in range(GROUP):
                    j = g * GROUP + b
                    last = nc.tensor.transpose(bank[3][:, b * P:(b + 1) * P], own[:, j, LEFT:LEFT + 1].broadcast_to([P, P]),
                                               ident[:, :])
                last.then_inc(sl_spread, 1)

            def transpose_tile(s, t):
                n = s * TILES + t
                pe.wait_ge(adj_loaded[t // LOAD], 16 * (s + 1))
                if not isinstance(n, int) or n >= RING:
                    pe.wait_ge(e_ready, n - RING + 1)
                for b in range(TB):
                    for r in range(RB):
                        c0 = (t % LOAD) * TW + b * P
                        last = nc.tensor.transpose(staged[t % RING][:, b, r * P:(r + 1) * P],
                                                   adj_b[:, t // LOAD, r, c0:c0 + P], ident_b[:, :])
                last.then_inc(tile_transposed, 1)

            def sum_tile(s, t):
                n = s * TILES + t
                pe.wait_ge(adjT_ready, n + 1)
                pe.wait_ge(e_hi_ready, n + 1)
                pe.wait_ge(e_lo_ready, n + 1)
                for r in range(RB):
                    if t == 0 and later(s):
                        pe.wait_ge(conv_ready[r], s)
                        pe.wait_ge(att_sum_ready[r], s)
                    elif t == 0 and r == RB - 1:
                        pe.wait_ge(sl_taken, GROUPS)
                    rows = slice(r * P, (r + 1) * P)
                    for b in range(TB):
                        j = t * TB + b
                        first, final = t == 0 and b == 0, t == TILES - 1 and b == TB - 1
                        a = adjT[:, t % RING, b, rows]
                        nc.tensor.matmul(adj_acc[r][:, 0:SUM], a, g_hi[:, j, :], start=first, stop=False)
                        nc.tensor.matmul(adj_acc[r][:, 0:SUM], a, g_lo[:, j, :], start=False, stop=final)
                        hi, lo = e_hi[:, t % RING, b, rows], e_lo[:, t % RING, b, rows]
                        nc.tensor.matmul(att_acc[r][:, 0:SUM], hi, h_hi[:, j, :], start=first, stop=False)
                        nc.tensor.matmul(att_acc[r][:, 0:D], hi, h_lo[:, j, :], start=False, stop=False)
                        last = nc.tensor.matmul(att_acc[r][:, 0:SUM], lo, h_hi[:, j, :], start=False, stop=final)
                    if t == TILES - 1 and r < RB - 1:
                        last.then_inc(rows_summed[r], 1)
                last.then_inc(tile_summed, 1)

            transpose_tokens(0)
            pe.wait_ge(w_lo_ready, 2)
            products(0, 1)
            transpose_tokens(1)
            products(2, 3, 4)
            spread_sl(0)
            products(5, 6)
            transpose_tokens(2)
            products(7, 8)
            spread_sl(1)
            pe.wait_ge(hnT_lo_ready, DC * (GROUPS - 1))
            pe.wait_ge(ident_b_ready, 1)
            transpose_tile(0, 0)
            products(9, 10)
            transpose_tokens(3)
            products(11)
            transpose_tile(0, 1)
            products(12)
            spread_sl(2)
            pe.wait_ge(hnT_lo_ready, DC * GROUPS)
            products(13)
            transpose_tile(0, 2)
            products(14)
            transpose_tile(0, 3)
            products(15)
            spread_sl(3)
            pe.wait_ge(consts_ready, 1)
            pe.wait_ge(unit_hi_taken, ALL_UNITS)
            pe.wait_ge(unit_lo_taken, ALL_UNITS)

            def sum_block(s):
                for t in range(TILES):
                    following = ahead_of(s, t, STAGE_AHEAD)
                    if not ended(*following):
                        transpose_tile(*following)
                    sum_tile(s, t)

            sum_block(0)
            with pe.Fori(1, BLOCKS - 1) as s:
                sum_block(s)
            sum_block(BLOCKS - 1)



_INS = ['x', 'adj', 'L0_gnn_W_sa', 'L0_gnn_a_sa', 'L0_gnn_W_gcnb', 'L0_gnn_b_gcnb', 'L0_gnn_Wa', 'L0_gnn_ba',
        'L0_gnn_Wb', 'L0_gnn_bb']


def kernel(**inputs):
    import numpy as _np
    import concourse.bacc as _bacc
    from concourse import mybir as _mybir
    from concourse.bass_utils import run_bass_kernel_spmd as _run

    nc = _bacc.Bacc("TRN2", target_bir_lowering=False, num_devices=1)
    arrays, args = {}, []
    for name in _INS:
        a = _np.ascontiguousarray(inputs[name])
        arrays[f"in_{name}_dram"] = a
        args.append(nc.dram_tensor(f"in_{name}_dram", a.shape, _mybir.dt.from_np(a.dtype), kind="ExternalInput").ap())
    args.append(nc.dram_tensor("out_0_dram", inputs['x'].shape, _mybir.dt.float32, kind="ExternalOutput").ap())
    graph_layer(nc, *args)
    r = _run(nc, [arrays], core_ids=[0])
    return r.results[0]["out_0_dram"]
```

```python
import concourse.bass as bass
from concourse import mybir
from contextlib import ExitStack

P = 128


def graph_layer(nc, x, adj, w_sa, a_sa, w_gcnb, b_gcnb, wa, ba, wb, bb, out):
    f32, f32r = mybir.dt.float32, mybir.dt.float32r
    bf16, u16 = mybir.dt.bfloat16, mybir.dt.uint16
    ALU, ACT = mybir.AluOpType, mybir.ActivationFunctionType

    N, D = x.shape
    LN_EPS, DEN_EPS, SLOPE = 1e-5, 1e-5, 0.01
    DC = D // P
    JB = N // P
    GROUP = 4
    GROUPS = JB // GROUP
    GW = GROUP * P
    RB = 2
    ROWS = RB * P
    BLOCKS = N // ROWS
    TB = 2
    TW = TB * P
    TILES = N // TW
    LOAD = 2
    LOADS = TILES // LOAD
    SUM = D + 2
    GATE = D
    SELF = D + 2
    RIGHT99, RIGHT01, LEFT = 2, 3, 4
    OWN = 6
    CAT = SELF + OWN
    CLEAR_AHEAD = 2
    RING = 4
    ERING = 4
    STAGE_AHEAD = 4
    STAGE_AT_ONCE = 2
    TAKE = 2
    WEIGH = 3
    BLEND = 4
    SQUASH = 5
    STORE = 6
    UNIT_BANKS = 4
    SPREAD_AFTER = [4, 8, 12, 15]
    X_LOADS = [GROUP // 2, GROUP // 2] + [GROUP] * (GROUPS - 1)
    WARM = 18
    assert TILES % RING == 0 and TAKE < RING == STAGE_AHEAD and STORE + 1 < TILES
    assert TILES % STAGE_AT_ONCE == 0 and N == BLOCKS * ROWS

    with ExitStack() as ctx:
        def sb(name, shape, dt=f32):
            return ctx.enter_context(nc.sbuf_tensor(name, [P] + shape, dt))

        def sem(name):
            return ctx.enter_context(nc.semaphore(name))

        BIAS_LOADS = 3
        ident = sb("ident", [P])
        ident_b = sb("ident_b", [P], bf16)
        x_sb = sb("x_sb", [JB, D])
        stats = sb("stats", [JB, 6])
        mean_var = sb("mean_var", [JB, 2])
        std = sb("std", [JB])
        rstd = sb("rstd", [JB])
        neg_mean_rstd = sb("neg_mean_rstd", [JB])
        warm = sb("warm", [1])
        xn = sb("xn", [2, GROUP, D])
        hnT_hi = sb("hnT_hi", [2, DC, GW], f32r)
        hnT_lo = sb("hnT_lo", [2, DC, GW], f32r)
        w_sa_sb = sb("w_sa_sb", [DC, D])
        w_sa_hi = sb("w_sa_hi", [DC, D], f32r)
        w_sa_lo = sb("w_sa_lo", [DC, D], f32r)
        w_cat = sb("w_cat", [DC, CAT])
        w_cat_hi = sb("w_cat_hi", [DC, CAT], f32r)
        w_cat_lo = sb("w_cat_lo", [DC, CAT], f32r)
        gate_rows = sb("gate_rows", [D])
        a_all = sb("a_all", [2 * D])
        b_all = sb("b_all", [SUM])
        own_bias = sb("own_bias", [OWN])
        dot_junk = sb("dot_junk", [D])
        neg_v = sb("neg_v", [DC, 2])
        neg_sl = sb("neg_sl", [N])
        neg_sl01 = sb("neg_sl01", [N])
        own = sb("own", [JB, OWN])
        g_hi = sb("g_hi", [JB, SUM], f32r)
        g_lo = sb("g_lo", [JB, SUM], f32r)
        h_hi = sb("h_hi", [JB, SUM], f32r)
        h_lo = sb("h_lo", [JB, D], f32r)

        adj_sb = sb("adj_sb", [LOADS, RB, LOAD * TW])
        score = sb("score", [RING, TB, ROWS])
        e = sb("e", [ERING, TB, ROWS])
        adjT = sb("adjT", [RING, TB, ROWS], f32r)
        e_hi = sb("e_hi", [RING, TB, ROWS], f32r)
        e_lo = sb("e_lo", [RING, TB, ROWS], f32r)

        conv = sb("conv", [RB, SUM])
        att_sum = sb("att_sum", [RB, SUM])
        logit = sb("logit", [RB, 2])
        exp_neg = sb("exp_neg", [RB, 2])
        one_plus = sb("one_plus", [RB, 2])
        gate = sb("gate", [RB, 2])
        den = sb("den", [RB])
        inv_den = sb("inv_den", [RB])
        att_scale = sb("att_scale", [RB])
        conv_gated = sb("conv_gated", [RB, D])
        mixed = sb("mixed", [RB, D])
        sig = sb("sig", [RB, D])
        y = sb("y", [RB, D])

        bank = [ctx.enter_context(nc.psum_tensor(f"bank{i}", [P, 512], f32)) for i in range(8)]
        adj_acc, att_acc = bank[0:RB], bank[RB:2 * RB]
        staged = [bank[4 + i][:, :].bitcast(bf16)[:, 0:TB * ROWS].rearrange("p (b r) -> p b r", b=TB)
                  for i in range(RING)]
        adj_b = adj_sb[:, :, :, :].bitcast(bf16).rearrange("p q r (j two) -> p q r j two", two=2)[:, :, :, :, 1]

        x_loaded = [sem(f"x_loaded{i}") for i in range(len(X_LOADS))]
        w_sa_loaded = sem("w_sa_loaded")
        a_loaded = sem("a_loaded")
        w_gcnb_loaded = sem("w_gcnb_loaded")
        bias_loaded = sem("bias_loaded")
        rows_loaded = sem("rows_loaded")
        adj_loaded = [sem(f"adj_loaded{q}") for q in range(LOADS)]
        ident_cleared = sem("ident_cleared")
        ident_ready = sem("ident_ready")
        ident_b_ready = sem("ident_b_ready")
        consts_ready = sem("consts_ready")
        dve_steps = sem("dve_steps")
        stats_ready = sem("stats_ready")
        var_ready = sem("var_ready")
        std_ready = sem("std_ready")
        rstd_ready = sem("rstd_ready")
        xn_ready = [sem(f"xn_ready{h}") for h in range(2)]
        gate_cols_ready = sem("gate_cols_ready")
        w_cat_ready = sem("w_cat_ready")
        w_sa_hi_ready = sem("w_sa_hi_ready")
        w_cat_hi_ready = sem("w_cat_hi_ready")
        w_sa_lo_ready = sem("w_sa_lo_ready")
        w_cat_lo_ready = sem("w_cat_lo_ready")
        xn_transposed = sem("xn_transposed")
        hnT_hi_ready = sem("hnT_hi_ready")
        hnT_lo_ready = sem("hnT_lo_ready")
        unit_done = sem("unit_done")
        unit_hi_taken = sem("unit_hi_taken")
        unit_lo_taken = sem("unit_lo_taken")
        own_ready = sem("own_ready")
        sl_spread = sem("sl_spread")
        sl_taken = sem("sl_taken")
        sl01_ready = sem("sl01_ready")

        arg_ready = sem("arg_ready")
        exp_ready = sem("exp_ready")
        e_zeroed = sem("e_zeroed")
        tile_transposed = sem("tile_transposed")
        adjT_ready = sem("adjT_ready")
        e_ready = sem("e_ready")
        e_hi_ready = sem("e_hi_ready")
        e_lo_ready = sem("e_lo_ready")
        tile_summed = sem("tile_summed")
        adj_summed = [sem(f"adj_summed{r}") for r in range(RB)]
        att_summed = [sem(f"att_summed{r}") for r in range(RB - 1)]
        conv_ready = [sem(f"conv_ready{r}") for r in range(RB)]
        att_sum_ready = [sem(f"att_sum_ready{r}") for r in range(RB)]
        logit_ready = sem("logit_ready")
        exp_neg_ready = sem("exp_neg_ready")
        den_ready = sem("den_ready")
        inv_den_ready = sem("inv_den_ready")
        one_plus_ready = sem("one_plus_ready")
        gate_ready = sem("gate_ready")
        att_scale_ready = sem("att_scale_ready")
        conv_gated_ready = sem("conv_gated_ready")
        mixed_ready = sem("mixed_ready")
        tanh_ready = sem("tanh_ready")
        sig_ready = sem("sig_ready")
        y_ready = sem("y_ready")
        shifted = sem("shifted")
        last_y_ready = [sem(f"last_y_ready{r}") for r in range(RB)]
        stored = sem("stored")

        ALL_UNITS = 2 * JB
        ALL_ROWS = slice(0, RB)

        def later(s):
            return not isinstance(s, int) or s > 0

        def apart(engine, value):
            value = value if isinstance(value, int) else engine.to_reg(value)
            engine.wait_ge(ident_ready, 1)
            return value

        def body(s, ahead):
            return [(s, t) for t in range(ahead, TILES)] + [(s + 1, t) for t in range(ahead)]

        def ahead_of(s, t, k):
            return (s, t + k) if t + k < TILES else (s + 1, t + k - TILES)

        CAT_PARTS = [slice(0, D), slice(D, CAT)]

        def x_load(b):
            return next(i for i in range(len(X_LOADS)) if b < sum(X_LOADS[:i + 1]))

        def unit_bank(u):
            return bank[(u + sum(u >= 2 * (j + 1) for j in SPREAD_AFTER)) % UNIT_BANKS]

        def spread_bank(g):
            return bank[(2 * (SPREAD_AFTER[g] + 1) + g) % UNIT_BANKS]

        def halves(g):
            return [range(g * GROUP + h * GROUP // 2, g * GROUP + (h + 1) * GROUP // 2) for h in range(2)]

        def ended(s, t):
            return isinstance(s, int) and s >= BLOCKS

        x_rows = x.rearrange("(b p) d -> p b d", p=P)
        adj_rows = adj.rearrange("(s r p) j -> s p r j", p=P, r=RB)
        out_rows = out.rearrange("(s r p) d -> s p r d", p=P, r=RB)

        block = ctx.enter_context(nc.Block())

        @block.sync
        def _(sp):
            def load_x(i):
                blocks = slice(sum(X_LOADS[:i]), sum(X_LOADS[:i + 1]))
                sp.dma_start(x_sb[:, blocks, :], x_rows[:, blocks, :]).then_inc(x_loaded[i], 16)

            load_x(0)
            load_x(1)
            sp.dma_start(w_sa_sb[:, :, :], w_sa.rearrange("(c p) n -> p c n", p=P)).then_inc(w_sa_loaded, 16)
            sp.dma_start(a_all[:, :], a_sa.broadcast_to([P, 2 * D])).then_inc(a_loaded, 16)
            sp.dma_start(w_cat[:, :, 0:D], w_gcnb.rearrange("(c p) n -> p c n", p=P)).then_inc(w_gcnb_loaded, 16)
            for i in range(2, len(X_LOADS)):
                load_x(i)

            def load(s, q):
                cols = slice(q * LOAD * TW, (q + 1) * LOAD * TW)
                sp.dma_start(adj_sb[:, q, :, :], adj_rows[s, :, :, cols]).then_inc(adj_loaded[q], 16)

            def store(s):
                sp.wait_ge(y_ready, s + 1)
                sp.dma_start(out_rows[s], y[:, :, :]).then_inc(stored, 16)

            def load_block(s):
                for q in range(LOADS):
                    sp.wait_ge(tile_transposed, TILES * (s - 1) + LOAD * (q + 1))
                    load(s, q)

            for q in range(LOADS):
                load(0, q)
            load_block(1)
            with sp.Fori(2, BLOCKS) as s:
                load_block(s)
                store(s - 2)
            store(BLOCKS - 2)
            for r in range(RB):
                sp.wait_ge(last_y_ready[r], 1)
                sp.dma_start(out_rows[BLOCKS - 1][:, r, :], y[:, r, :]).then_inc(stored, 16)
            sp.wait_ge(stored, 16 * (BLOCKS - 1 + RB))

        @block.gpsimd
        def _(pool):
            nc.gpsimd.memset(ident[:, :], 0.0).then_inc(ident_cleared, 1)
            pool.wait_ge(ident_cleared, 1)
            nc.gpsimd.affine_select(out=ident[:, :], in_=ident[:, :], compare_op=ALU.not_equal, fill=1.0,
                                    base=0, pattern=[[-1, P]], channel_multiplier=1).then_inc(ident_ready, 1)
            nc.gpsimd.memset(h_hi[:, :, D:D + 1].bitcast(f32), 1.0)
            nc.gpsimd.memset(h_hi[:, :, D + 1:SUM].bitcast(f32), 0.0)
            nc.gpsimd.memset(b_all[:, D:SUM], 0.0)
            nc.gpsimd.memset(w_cat[:, :, CAT - 1:CAT], 0.0)
            nc.gpsimd.memset(own_bias[:, 2:OWN], 0.0).then_inc(consts_ready, 1)
            pool.wait_ge(ident_ready, 1)
            nc.gpsimd.tensor_copy(ident_b[:, :], ident[:, :]).then_inc(ident_b_ready, 1)

            def normalise(g, half):
                pool.wait_ge(rstd_ready, g + 1)
                if g >= 2:
                    pool.wait_ge(xn_transposed, DC * (g - 1))
                for b in halves(g)[half]:
                    last = nc.gpsimd.tensor_scalar(xn[:, g % 2, b % GROUP, :], x_sb[:, b, :], rstd[:, b:b + 1],
                                                   neg_mean_rstd[:, b:b + 1], ALU.mult, ALU.add)
                last.then_inc(xn_ready[half], 1)

            def scale_sl(g):
                pool.wait_ge(sl_taken, g + 1)
                tokens = slice(g * GW, (g + 1) * GW)
                nc.gpsimd.tensor_scalar(neg_sl01[:, tokens], neg_sl[:, tokens], SLOPE, 0.0,
                                        ALU.mult, ALU.add).then_inc(sl01_ready, 1)

            def clear(s, t):
                n = s * TILES + t
                used = apart(pool, n - ERING + 1)
                if later(s) or t >= ERING:
                    pool.wait_ge(e_lo_ready, used)
                nc.gpsimd.memset(e[:, t % ERING], 0.0).then_inc(e_zeroed, 1)

            def step(s, t):
                following = ahead_of(s, t, CLEAR_AHEAD)
                if not ended(*following):
                    clear(*following)
                pool.wait_ge(e_hi_ready, s * TILES + t + 1)
                nc.gpsimd.tensor_tensor(e_lo[:, t % RING], e[:, t % ERING], e_hi[:, t % RING].bitcast(f32),
                                        ALU.subtract).then_inc(e_lo_ready, 1)

            def finish(s):
                count = apart(pool, s + 1)
                pool.wait_ge(tanh_ready, count)
                nc.gpsimd.tensor_scalar(sig[:, :, :], sig[:, :, :], 0.5, 0.5, ALU.mult,
                                        ALU.add).then_inc(sig_ready, 1)
                pool.wait_ge(sig_ready, s + 1)
                if later(s):
                    pool.wait_ge(stored, 16 * s)
                nc.gpsimd.tensor_tensor(y[:, :, :], sig[:, :, :], x_sb[:, bass.ds(s * RB, RB), :],
                                        ALU.add).then_inc(y_ready, 1)

            def split_w_sa(c):
                pool.wait_ge(w_sa_hi_ready, 1)
                nc.gpsimd.tensor_tensor(w_sa_lo[:, c, :], w_sa_sb[:, c, :], w_sa_hi[:, c, :].bitcast(f32),
                                        ALU.subtract).then_inc(w_sa_lo_ready, 1)

            def split_w_cat(part):
                pool.wait_ge(w_cat_hi_ready, part + 1)
                cols = CAT_PARTS[part]
                nc.gpsimd.tensor_tensor(w_cat_lo[:, :, cols], w_cat[:, :, cols], w_cat_hi[:, :, cols].bitcast(f32),
                                        ALU.subtract).then_inc(w_cat_lo_ready, 1)

            split_w_sa(0)
            normalise(0, 1)
            split_w_cat(0)
            for c in range(1, DC):
                split_w_sa(c)
            split_w_cat(1)
            normalise(1, 1)
            for t in range(CLEAR_AHEAD):
                clear(0, t)
            for g in range(2, GROUPS):
                for half in range(2):
                    normalise(g, half)
                scale_sl(g - 2)
            step(0, 0)
            scale_sl(GROUPS - 2)
            step(0, 1)
            scale_sl(GROUPS - 1)
            for t in range(2, STORE + 1):
                step(0, t)
            for at, t in body(0, STORE + 1):
                step(at, t)
            finish(0)
            with pool.Fori(1, BLOCKS - 1) as s:
                for at, t in body(s, STORE + 1):
                    step(at, t)
                finish(s)
            for t in range(STORE + 1, TILES):
                step(BLOCKS - 1, t)
            nc.gpsimd.tensor_scalar(x_sb[:, JB - RB:JB, :], x_sb[:, JB - RB:JB, :], 1.0, 0.5,
                                    ALU.mult, ALU.add).then_inc(shifted, 1)

        @block.scalar
        def _(act):
            act.dma_start(gate_rows[0:2, :], wa.rearrange("o (h d) -> (o h) d", h=2)).then_inc(rows_loaded, 16)
            act.dma_start(gate_rows[2:4, :], wb.rearrange("o (h d) -> (o h) d", h=2)).then_inc(rows_loaded, 16)
            act.wait_ge(ident_ready, 1)
            nc.scalar.activation(warm[:, :], ident[:, 0:1], ACT.Sqrt, bias=LN_EPS)
            act.dma_start(own_bias[:, 0:1], ba.unsqueeze(0).broadcast_to([P, 1])).then_inc(bias_loaded, 16)
            act.dma_start(own_bias[:, 1:2], bb.unsqueeze(0).broadcast_to([P, 1])).then_inc(bias_loaded, 16)
            act.dma_start(b_all[:, 0:D], b_gcnb.unsqueeze(0).broadcast_to([P, D])).then_inc(bias_loaded, 16)

            def standard_deviation(g):
                act.wait_ge(var_ready, g + 1)
                tokens = slice(g * GROUP, (g + 1) * GROUP)
                nc.scalar.activation(std[:, tokens], mean_var[:, tokens, 1], ACT.Sqrt,
                                     bias=LN_EPS).then_inc(std_ready, 1)

            def normalise(g):
                act.wait_ge(rstd_ready, g + 1)
                for b in halves(g)[0]:
                    last = nc.scalar.activation(xn[:, g % 2, b % GROUP, :], x_sb[:, b, :], ACT.Identity,
                                                bias=neg_mean_rstd[:, b:b + 1], scale=rstd[:, b:b + 1])
                last.then_inc(xn_ready[0], 1)

            def hidden_hi(g, *chunks):
                for c in chunks:
                    act.wait_ge(xn_transposed, g * DC + c + 1)
                    if g >= 2:
                        act.wait_ge(unit_done, 2 * GROUP * (g - 1))
                    nc.scalar.activation(hnT_hi[:, g % 2, c, :], bank[4 + DC * (g % 2) + c][:, :],
                                         ACT.Relu).then_inc(hnT_hi_ready, 1)

            def products_hi(*blocks):
                for j in blocks:
                    u = 2 * j
                    act.wait_ge(unit_done, u + 1)
                    nc.scalar.activation(g_hi[:, j, :], unit_bank(u)[:, 0:SUM],
                                         ACT.Copy).then_inc(unit_hi_taken, 1)
                    u += 1
                    act.wait_ge(unit_done, u + 1)
                    nc.scalar.activation(h_hi[:, j, 0:D], unit_bank(u)[:, 0:D],
                                         ACT.Copy).then_inc(unit_hi_taken, 1)

            def take_sl(g):
                act.wait_ge(sl_spread, g + 1)
                nc.scalar.activation(neg_sl[:, g * GW:(g + 1) * GW], spread_bank(g)[:, :], ACT.Copy).then_inc(sl_taken, 1)

            def exponential(s, t):
                act.wait_ge(arg_ready, s * TILES + t + 1)
                for b in range(TB):
                    j = t * TB + b
                    last = nc.scalar.activation(score[:, t % RING, b, :], score[:, t % RING, b, :], ACT.Exp,
                                                bias=own[:, j, RIGHT01:RIGHT01 + 1])
                last.then_inc(exp_ready, 1)

            def take_adj(s, t):
                n = s * TILES + t
                act.wait_ge(tile_transposed, n + 1)
                if not isinstance(n, int) or n >= RING:
                    act.wait_ge(tile_summed, n - RING + 1)
                nc.scalar.activation(adjT[:, t % RING], staged[t % RING], ACT.Copy).then_inc(adjT_ready, 1)

            def high_part(s, t):
                act.wait_ge(e_ready, s * TILES + t + 1)
                nc.scalar.activation(e_hi[:, t % RING], e[:, t % ERING], ACT.Copy).then_inc(e_hi_ready, 1)

            def step(s, t):
                following = ahead_of(s, t, 1)
                if not ended(*following):
                    exponential(*following)
                    take_adj(*following)
                high_part(s, t)

            def take_sums(s, blocks=range(RB)):
                if later(s):
                    act.wait_ge(mixed_ready, s)
                for r in blocks:
                    if r < RB - 1:
                        act.wait_ge(att_summed[r], s + 1)
                    else:
                        act.wait_ge(tile_summed, TILES * (s + 1))
                    nc.scalar.activation(att_sum[:, r, :], att_acc[r][:, 0:SUM],
                                         ACT.Copy).then_inc(att_sum_ready[r], 1)

            def gate_exponential(s, rows=ALL_ROWS, part=0):
                act.wait_ge(logit_ready, s + part + 1)
                nc.scalar.activation(exp_neg[:, rows, :], logit[:, rows, :], ACT.Exp,
                                     scale=-1.0).then_inc(exp_neg_ready, 1)

            def squash(s, rows=ALL_ROWS, part=0):
                act.wait_ge(mixed_ready, s + part + 1)
                if later(s):
                    act.wait_ge(y_ready, s)
                nc.scalar.activation(sig[:, rows, :], mixed[:, rows, :], ACT.Tanh, scale=0.5).then_inc(tanh_ready, 1)

            def run(s):
                for at, t in body(s, SQUASH + 1):
                    if t == TAKE:
                        exponential(at, t + 1)
                        take_sums(s, [0])
                        high_part(at, t)
                        take_sums(s, range(1, RB))
                        take_adj(at, t + 1)
                        gate_exponential(s)
                    else:
                        step(at, t)
                squash(s)

            act.wait_ge(w_sa_loaded, 16)
            nc.scalar.activation(w_sa_hi[:, :, :], w_sa_sb[:, :, :], ACT.Copy).then_inc(w_sa_hi_ready, 1)
            standard_deviation(0)
            normalise(0)
            act.wait_ge(w_gcnb_loaded, 16)
            nc.scalar.activation(w_cat_hi[:, :, CAT_PARTS[0]], w_cat[:, :, CAT_PARTS[0]],
                                 ACT.Copy).then_inc(w_cat_hi_ready, 1)
            hidden_hi(0, 0)
            act.wait_ge(w_cat_ready, 1)
            nc.scalar.activation(w_cat_hi[:, :, CAT_PARTS[1]], w_cat[:, :, CAT_PARTS[1]],
                                 ACT.Copy).then_inc(w_cat_hi_ready, 1)
            hidden_hi(0, 1)
            standard_deviation(1)
            normalise(1)
            products_hi(0, 1)
            standard_deviation(2)
            hidden_hi(1, 0, 1)
            products_hi(2, 3, 4)
            take_sl(0)
            products_hi(5)
            hidden_hi(2, 0, 1)
            products_hi(6)
            standard_deviation(3)
            products_hi(7)
            nc.scalar.activation(warm[:, :], ident[:, 0:1], ACT.Exp)
            products_hi(8)
            take_sl(1)
            exponential(0, 0)
            products_hi(9)
            take_adj(0, 0)
            hidden_hi(3, 0, 1)
            products_hi(10)
            exponential(0, 1)
            products_hi(11)
            high_part(0, 0)
            products_hi(12)
            take_sl(2)
            take_adj(0, 1)
            products_hi(13)
            exponential(0, 2)
            products_hi(14, 15)
            take_sl(3)
            high_part(0, 1)
            take_adj(0, 2)
            for t in range(2, SQUASH + 1):
                step(0, t)
            run(0)
            with act.Fori(1, BLOCKS - 1) as s:
                run(s)
            for t in range(SQUASH + 1, TILES):
                step(BLOCKS - 1, t)
            for r in range(RB):
                take_sums(BLOCKS - 1, [r])
                gate_exponential(BLOCKS - 1, slice(r, r + 1), r)
            for r in range(RB):
                squash(BLOCKS - 1, slice(r, r + 1), r)

        @block.vector
        def _(dve):
            links = [0]

            def link(ins):
                links[0] += 1
                ins.then_inc(dve_steps, 1)
                dve.wait_ge(dve_steps, links[0])

            def measure(b):
                dve.wait_ge(x_loaded[x_load(b)], 16)
                nc.vector.bn_stats(stats[:, b, :], x_sb[:, b, :]).then_inc(stats_ready, 1)

            def variance(g):
                dve.wait_ge(stats_ready, (g + 1) * GROUP)
                for b in range(g * GROUP, (g + 1) * GROUP):
                    last = nc.vector.bn_aggr(mean_var[:, b, :], stats[:, b, :])
                last.then_inc(var_ready, 1)

            def inverse_deviation(g):
                blocks = slice(g * GROUP, (g + 1) * GROUP)
                dve.wait_ge(std_ready, g + 1)
                link(nc.vector.reciprocal(rstd[:, blocks], std[:, blocks]))
                nc.vector.scalar_tensor_tensor(neg_mean_rstd[:, blocks], mean_var[:, blocks, 0], -1.0, rstd[:, blocks],
                                               ALU.mult, ALU.mult).then_inc(rstd_ready, 1)

            def hidden_lo(g, *chunks):
                for c in chunks:
                    dve.wait_ge(hnT_hi_ready, g * DC + c + 1)
                    nc.vector.scalar_tensor_tensor(hnT_lo[:, g % 2, c, :], bank[4 + DC * (g % 2) + c][:, :], 0.0,
                                                   hnT_hi[:, g % 2, c, :].bitcast(f32), ALU.max,
                                                   ALU.subtract).then_inc(hnT_lo_ready, 1)

            def products_lo(*blocks):
                for j in blocks:
                    u = 2 * j
                    dve.wait_ge(unit_hi_taken, u + 1)
                    nc.vector.tensor_tensor(own[:, j, :], unit_bank(u)[:, SELF:CAT], own_bias[:, :],
                                            ALU.add).then_inc(own_ready, 1)
                    nc.vector.tensor_tensor(g_lo[:, j, :], unit_bank(u)[:, 0:SUM],
                                            g_hi[:, j, :].bitcast(f32), ALU.subtract).then_inc(unit_lo_taken, 1)
                    u += 1
                    dve.wait_ge(unit_hi_taken, u + 1)
                    nc.vector.tensor_tensor(h_lo[:, j, :], unit_bank(u)[:, 0:D],
                                            h_hi[:, j, 0:D].bitcast(f32), ALU.subtract).then_inc(unit_lo_taken, 1)

            def argument(s, t):
                if later(s) or t >= RING:
                    dve.wait_ge(e_ready, s * TILES + t - RING + 1)
                rows = bass.ds(s * ROWS, ROWS)
                for b in range(TB):
                    j = t * TB + b
                    last = nc.vector.scalar_tensor_tensor(score[:, t % RING, b, :], neg_sl[:, rows],
                                                          own[:, j, RIGHT99:RIGHT99 + 1], neg_sl01[:, rows],
                                                          ALU.add, ALU.min)
                last.then_inc(arg_ready, 1)

            def select(s, t):
                n = s * TILES + t
                count = apart(dve, n + 1)
                dve.wait_ge(exp_ready, count)
                dve.wait_ge(e_zeroed, count)
                dve.wait_ge(adjT_ready, count)
                nc.vector.copy_predicated(e[:, t % ERING], staged[t % RING].bitcast(u16),
                                          score[:, t % RING]).then_inc(e_ready, 1)

            def next_argument(s, t):
                following = ahead_of(s, t, 2)
                if not ended(*following):
                    argument(*following)

            def step(s, t):
                select(s, t)
                next_argument(s, t)

            def take_sums(s, rows=ALL_ROWS, part=0):
                blocks = range(rows.start, rows.stop)
                if later(s):
                    dve.wait_ge(conv_gated_ready, s)
                for r in blocks:
                    dve.wait_ge(adj_summed[r], s + 1)
                    nc.vector.tensor_tensor(conv[:, r, :], adj_acc[r][:, 0:SUM], b_all[:, :],
                                            ALU.add).then_inc(conv_ready[r], 1)
                for r in blocks:
                    dve.wait_ge(conv_ready[r], s + 1)
                nc.vector.tensor_tensor(logit[:, rows, :], conv[:, rows, GATE:GATE + 2],
                                        own[:, bass.ds(s * RB + rows.start, len(blocks)), 0:2],
                                        ALU.add).then_inc(logit_ready, 1)

            def weigh(s, rows=ALL_ROWS, part=0):
                count = s + part + 1
                for r in range(rows.start, rows.stop):
                    dve.wait_ge(att_sum_ready[r], s + 1)
                nc.vector.tensor_scalar(den[:, rows], att_sum[:, rows, D], DEN_EPS, None,
                                        ALU.add).then_inc(den_ready, 1)
                dve.wait_ge(exp_neg_ready, count)
                nc.vector.tensor_scalar(one_plus[:, rows, :], exp_neg[:, rows, :], 1.0, None,
                                        ALU.add).then_inc(one_plus_ready, 1)
                dve.wait_ge(den_ready, count)
                nc.vector.reciprocal(inv_den[:, rows], den[:, rows]).then_inc(inv_den_ready, 1)
                dve.wait_ge(one_plus_ready, count)
                nc.vector.reciprocal(gate[:, rows, :], one_plus[:, rows, :]).then_inc(gate_ready, 1)
                dve.wait_ge(gate_ready, count)
                dve.wait_ge(inv_den_ready, count)
                nc.vector.tensor_tensor(att_scale[:, rows], gate[:, rows, 0], inv_den[:, rows],
                                        ALU.mult).then_inc(att_scale_ready, 1)

            def blend(s, rows=ALL_ROWS, part=0):
                count = s + part + 1
                blocks = range(rows.start, rows.stop)
                for r in blocks:
                    last = nc.vector.tensor_scalar(conv_gated[:, r, :], conv[:, r, 0:D], gate[:, r, 1:2], None,
                                                   ALU.mult)
                last.then_inc(conv_gated_ready, 1)
                dve.wait_ge(conv_gated_ready, count)
                dve.wait_ge(att_scale_ready, count)
                if later(s):
                    dve.wait_ge(tanh_ready, s)
                for r in blocks:
                    last = nc.vector.scalar_tensor_tensor(mixed[:, r, :], att_sum[:, r, 0:D], att_scale[:, r:r + 1],
                                                          conv_gated[:, r, :], ALU.mult, ALU.add)
                last.then_inc(mixed_ready, 1)

            def run(s):
                for at, t in body(s, BLEND + 1):
                    select(at, t)
                    if t == TAKE:
                        take_sums(s)
                    next_argument(at, t)
                    if t == WEIGH:
                        weigh(s)
                blend(s)

            for b in range(GROUP):
                measure(b)
            variance(0)
            inverse_deviation(0)
            dve.wait_ge(w_sa_loaded, 16)
            dve.wait_ge(a_loaded, 16)
            for c in range(DC):
                for k in range(2):
                    link(nc.vector.tensor_tensor_reduce(out=dot_junk[:, :], in0=w_sa_sb[:, c, :],
                                                        in1=a_all[:, k * D:(k + 1) * D], scale=-1.0, scalar=0.0,
                                                        op0=ALU.mult, op1=ALU.add,
                                                        accum_out=neg_v[:, c, k:k + 1]))
            for at, k, share in ((LEFT, 0, 1.0), (RIGHT99, 1, 1.0 - SLOPE), (RIGHT01, 1, SLOPE)):
                nc.vector.tensor_scalar(w_cat[:, :, SELF + at:SELF + at + 1], neg_v[:, :, k:k + 1], share, None,
                                        ALU.mult)
            dve.wait_ge(consts_ready, 1)
            dve.wait_ge(gate_cols_ready, 1)
            nc.vector.tensor_copy(w_cat[:, :, GATE:GATE + 4].rearrange("p c (h w) -> p c h w", h=2),
                                  bank[3][:, 0:4 * DC].rearrange("p (c w h) -> p c h w", c=DC, w=2)
                                  ).then_inc(w_cat_ready, 1)
            measure(4)
            measure(5)
            hidden_lo(0, 0, 1)
            measure(6)
            measure(7)
            variance(1)
            measure(8)
            inverse_deviation(1)
            for b in range(9, 12):
                measure(b)
            dve.wait_ge(bias_loaded, 16 * BIAS_LOADS)
            products_lo(0)
            variance(2)
            products_lo(1)
            hidden_lo(1, 0, 1)
            products_lo(2)
            inverse_deviation(2)
            products_lo(3)
            measure(12)
            products_lo(4)
            measure(13)
            measure(14)
            products_lo(5)
            hidden_lo(2, 0, 1)
            measure(15)
            variance(3)
            products_lo(6)
            products_lo(7)
            inverse_deviation(3)
            dve.wait_ge(sl01_ready, 1)
            argument(0, 0)
            products_lo(8)
            argument(0, 1)
            products_lo(9)
            hidden_lo(3, 0, 1)
            products_lo(10)
            select(0, 0)
            argument(0, 2)
            products_lo(11)
            products_lo(12)
            select(0, 1)
            products_lo(13, 14, 15)
            argument(0, 3)
            for t in range(2, BLEND + 1):
                step(0, t)
            run(0)
            dve.wait_ge(sl01_ready, GROUPS)
            with dve.Fori(1, BLOCKS - 1) as s:
                run(s)
            for t in range(BLEND + 1, TILES):
                step(BLOCKS - 1, t)
            parts = [(slice(r, r + 1), r) for r in range(RB)]
            for rows, r in parts:
                take_sums(BLOCKS - 1, rows, r)
                if r:
                    blend(BLOCKS - 1, *parts[r - 1])
                weigh(BLOCKS - 1, rows, r)
            blend(BLOCKS - 1, *parts[-1])
            dve.wait_ge(shifted, 1)
            dve.wait_ge(stored, 16 * (BLOCKS - 1))
            for rows, r in parts:
                dve.wait_ge(tanh_ready, BLOCKS + r)
                nc.vector.scalar_tensor_tensor(y[:, r, :], sig[:, r, :], 0.5, x_sb[:, JB - RB + r, :],
                                               ALU.mult, ALU.add).then_inc(last_y_ready[r], 1)

        @block.tensor
        def _(pe):
            def keep_warm(products=WARM):
                for _ in range(products):
                    nc.tensor.transpose(bank[0][:, 0:P], ident[:, :], ident[:, :])

            pe.wait_ge(ident_ready, 1)
            keep_warm()
            pe.wait_ge(rows_loaded, 32)
            for c in range(DC):
                last = nc.tensor.transpose(bank[3][:, 4 * c:4 * c + 4], gate_rows[0:4, c * P:(c + 1) * P],
                                           ident[0:4, 0:4])
            last.then_inc(gate_cols_ready, 1)

            def transpose_tokens(g):
                for half in range(2):
                    pe.wait_ge(xn_ready[half], g + 1)
                if g >= 2:
                    pe.wait_ge(hnT_hi_ready, DC * (g - 1))
                    pe.wait_ge(hnT_lo_ready, DC * (g - 1))
                for c in range(DC):
                    for b in range(GROUP):
                        last = nc.tensor.transpose(bank[4 + DC * (g % 2) + c][:, b * P:(b + 1) * P],
                                                   xn[:, g % 2, b, c * P:(c + 1) * P], ident[:, :])
                    last.then_inc(xn_transposed, 1)

            def wait_bank_taken(used, u):
                units = [k for k in range(u) if unit_bank(k) is used]
                spreads = [g for g in range(GROUPS) if 2 * (SPREAD_AFTER[g] + 1) <= u and spread_bank(g) is used]
                if spreads and not (units and units[-1] >= 2 * (SPREAD_AFTER[spreads[-1]] + 1)):
                    pe.wait_ge(sl_taken, spreads[-1] + 1)
                elif units:
                    pe.wait_ge(unit_hi_taken, units[-1] + 1)
                    pe.wait_ge(unit_lo_taken, units[-1] + 1)

            def product(u, width, stationary, moving):
                wait_bank_taken(unit_bank(u), u)
                (s_hi, s_lo), (m_hi, m_lo) = stationary, moving
                for c in range(DC):
                    for i, (lhs, rhs) in enumerate(((s_hi, m_hi), (s_hi, m_lo), (s_lo, m_hi))):
                        last = nc.tensor.matmul(unit_bank(u)[:, 0:width], lhs[:, c, :], rhs[:, c, :],
                                                start=c == 0 and i == 0, stop=c == DC - 1 and i == 2)
                last.then_inc(unit_done, 1)

            def products(*blocks):
                for j in blocks:
                    g, b = j // GROUP, j % GROUP
                    if b == 0:
                        pe.wait_ge(hnT_hi_ready, DC * (g + 1))
                        pe.wait_ge(hnT_lo_ready, DC * (g + 1))
                    cols = slice(b * P, (b + 1) * P)
                    tokens = (hnT_hi[:, g % 2, :, cols], hnT_lo[:, g % 2, :, cols])
                    product(2 * j, CAT, tokens, (w_cat_hi, w_cat_lo))
                    product(2 * j + 1, D, tokens, (w_sa_hi, w_sa_lo))

            def spread_sl(g):
                pe.wait_ge(own_ready, GROUP * (g + 1))
                units = [k for k in range(2 * (SPREAD_AFTER[g] + 1)) if unit_bank(k) is spread_bank(g)]
                pe.wait_ge(unit_hi_taken, units[-1] + 1)
                pe.wait_ge(unit_lo_taken, units[-1] + 1)
                for b in range(GROUP):
                    j = g * GROUP + b
                    last = nc.tensor.transpose(spread_bank(g)[:, b * P:(b + 1) * P],
                                               own[:, j, LEFT:LEFT + 1].broadcast_to([P, P]), ident[:, :])
                last.then_inc(sl_spread, 1)

            def transpose_tile(s, t):
                n = s * TILES + t
                pe.wait_ge(adj_loaded[t // LOAD], 16 * (s + 1))
                if not isinstance(n, int) or n >= RING:
                    pe.wait_ge(e_ready, n - RING + 1)
                for b in range(TB):
                    for r in range(RB):
                        c0 = (t % LOAD) * TW + b * P
                        last = nc.tensor.transpose(staged[t % RING][:, b, r * P:(r + 1) * P],
                                                   adj_b[:, t // LOAD, r, c0:c0 + P], ident_b[:, :])
                last.then_inc(tile_transposed, 1)

            def sum_tile(s, t):
                n = s * TILES + t
                pe.wait_ge(e_lo_ready, n + 1)
                if t == 0 and not later(s):
                    pe.wait_ge(consts_ready, 1)
                    pe.wait_ge(unit_hi_taken, ALL_UNITS)
                    pe.wait_ge(unit_lo_taken, ALL_UNITS)
                for r in range(RB):
                    if t == 0 and later(s):
                        pe.wait_ge(conv_ready[r], s)
                        pe.wait_ge(att_sum_ready[r], s)
                    elif t == 0 and r == RB - 1:
                        pe.wait_ge(sl_taken, GROUPS)
                    rows = slice(r * P, (r + 1) * P)
                    steps = [(b, t * TB + b, t == 0 and b == 0, t == TILES - 1 and b == TB - 1) for b in range(TB)]
                    for b, j, first, final in steps:
                        a = adjT[:, t % RING, b, rows]
                        nc.tensor.matmul(adj_acc[r][:, 0:SUM], a, g_hi[:, j, :], start=first, stop=False)
                        last = nc.tensor.matmul(adj_acc[r][:, 0:SUM], a, g_lo[:, j, :], start=False, stop=final)
                    if t == TILES - 1:
                        last.then_inc(adj_summed[r], 1)
                    for b, j, first, final in steps:
                        hi, lo = e_hi[:, t % RING, b, rows], e_lo[:, t % RING, b, rows]
                        nc.tensor.matmul(att_acc[r][:, 0:SUM], hi, h_hi[:, j, :], start=first, stop=False)
                        nc.tensor.matmul(att_acc[r][:, 0:D], hi, h_lo[:, j, :], start=False, stop=False)
                        last = nc.tensor.matmul(att_acc[r][:, 0:SUM], lo, h_hi[:, j, :], start=False, stop=final)
                    if t == TILES - 1 and r < RB - 1:
                        last.then_inc(att_summed[r], 1)
                last.then_inc(tile_summed, 1)

            keep_warm(WARM * 2 // 3)
            transpose_tokens(0)
            keep_warm(WARM // 2)
            pe.wait_ge(w_sa_lo_ready, DC)
            pe.wait_ge(w_cat_lo_ready, 2)
            products(0, 1)
            transpose_tokens(1)
            products(2, 3, 4)
            spread_sl(0)
            products(5)
            transpose_tokens(2)
            products(6, 7)
            pe.wait_ge(ident_b_ready, 1)
            products(8)
            spread_sl(1)
            pe.wait_ge(hnT_lo_ready, DC * (GROUPS - 1))
            transpose_tile(0, 0)
            products(9)
            transpose_tokens(3)
            products(10, 11)
            transpose_tile(0, 1)
            products(12)
            spread_sl(2)
            pe.wait_ge(hnT_lo_ready, DC * GROUPS)
            products(13)
            transpose_tile(0, 2)
            products(14)
            transpose_tile(0, 3)
            products(15)
            spread_sl(3)

            def sum_block(s):
                for t in range(TILES):
                    if t % STAGE_AT_ONCE == 0:
                        for k in range(STAGE_AT_ONCE):
                            following = ahead_of(s, t, STAGE_AHEAD + k)
                            if not ended(*following):
                                transpose_tile(*following)
                    sum_tile(s, t)

            sum_block(0)
            with pe.Fori(1, BLOCKS - 1) as s:
                sum_block(s)
            sum_block(BLOCKS - 1)



_INS = ['x', 'adj', 'L0_gnn_W_sa', 'L0_gnn_a_sa', 'L0_gnn_W_gcnb', 'L0_gnn_b_gcnb', 'L0_gnn_Wa', 'L0_gnn_ba',
        'L0_gnn_Wb', 'L0_gnn_bb']


def kernel(**inputs):
    import numpy as _np
    import concourse.bacc as _bacc
    from concourse import mybir as _mybir
    from concourse.bass_utils import run_bass_kernel_spmd as _run

    nc = _bacc.Bacc("TRN2", target_bir_lowering=False, num_devices=1)
    arrays, args = {}, []
    for name in _INS:
        a = _np.ascontiguousarray(inputs[name])
        arrays[f"in_{name}_dram"] = a
        args.append(nc.dram_tensor(f"in_{name}_dram", a.shape, _mybir.dt.from_np(a.dtype), kind="ExternalInput").ap())
    args.append(nc.dram_tensor("out_0_dram", inputs['x'].shape, _mybir.dt.float32, kind="ExternalOutput").ap())
    graph_layer(nc, *args)
    r = _run(nc, [arrays], core_ids=[0])
    return r.results[0]["out_0_dram"]
```
